# Optimizing a Trainium2 kernel written in Bass

```python
import numpy as np
import jax
import jax.numpy as jnp

def _softmax(x, axis=-1):
    return jax.nn.softmax(x, axis=axis)

def _gelu(x):
    return jax.nn.gelu(x, approximate=True)

def _silu(x):
    return jax.nn.silu(x)

def _sigmoid(x):
    return jax.nn.sigmoid(x)

def _layernorm(x, axis=-1, eps=1e-05):
    m = jnp.mean(x, axis=axis, keepdims=True)
    v = jnp.var(x, axis=axis, keepdims=True)
    return (x - m) / jnp.sqrt(v + eps)

def _scatter_add(tgt, idx, src, axis=0):
    return tgt.at[idx].add(src)

def _segment_sum(src, seg, n):
    return jax.ops.segment_sum(src, seg, n)
kernel_name = 'mk_conv_seq_d4_conv_nchw512_r2_7fae48'

def setup_inputs(seed: int=0):
    np.random.seed(seed)
    _w = jnp.asarray

    def _rec_inputs():
        import jax
        import jax.numpy as jnp
        _gk = jax.random.key(seed)
        x = 7.22e-05 + 1 * jax.random.normal(jax.random.fold_in(_gk, 1), (4, 256, 32, 32), jnp.float32)
        return x
    x = _rec_inputs()

    def _L0_conv_setup():
        import jax, jax.numpy as jnp
        import numpy as np
        C_IN = 256
        MID = C_IN // 8
        B, H, W = (4, 32, 32)
        key = jax.random.key(seed)
        ks = jax.random.split(key, 7)
        s = 0.02
        return {'x': jax.random.normal(ks[0], (B, C_IN, H, W), dtype=jnp.float32), 'Wq': jax.random.normal(ks[1], (MID, C_IN), dtype=jnp.float32) * s, 'bq': jnp.zeros((MID,), dtype=jnp.float32), 'Wk': jax.random.normal(ks[2], (MID, C_IN), dtype=jnp.float32) * s, 'bk': jnp.zeros((MID,), dtype=jnp.float32), 'Wv': jax.random.normal(ks[3], (C_IN, C_IN), dtype=jnp.float32) * s, 'bv': jnp.zeros((C_IN,), dtype=jnp.float32), 'gamma': jnp.ones((1,), dtype=jnp.float32)}
    _L0_conv_all = _L0_conv_setup()
    _L0_conv_in = {k: v for k, v in _L0_conv_all.items() if k in ('Wq', 'bq', 'Wk', 'bk', 'Wv', 'bv', 'gamma')}
    del _L0_conv_all

    def _L1_conv_setup():
        import jax, jax.numpy as jnp
        import numpy as np
        NUM_GROUPS = 32
        EPS = 1e-06

        def group_norm(x, scale, bias):
            b, c, h, w = x.shape
            g = NUM_GROUPS
            xg = x.reshape(b, g, c // g, h, w)
            mean = xg.mean(axis=(2, 3, 4), keepdims=True)
            var = xg.var(axis=(2, 3, 4), keepdims=True)
            xg = (xg - mean) * jax.lax.rsqrt(var + EPS)
            x = xg.reshape(b, c, h, w)
            return x * scale[None, :, None, None] + bias[None, :, None, None]

        def conv1x1(x, w, b):
            return jnp.einsum('oc,bchw->bohw', w, x) + b[None, :, None, None]
        key = jax.random.key(seed)
        ks = jax.random.split(key, 6)
        B, C, H, W = (8, 256, 32, 32)
        s = 1.0 / np.sqrt(C)
        return {'x': jax.random.normal(ks[0], (B, C, H, W), dtype=jnp.float32), 'gn_scale': jnp.ones((C,), jnp.float32), 'gn_bias': jnp.zeros((C,), jnp.float32), 'wq': jax.random.normal(ks[1], (C, C), jnp.float32) * s, 'bq': jnp.zeros((C,), jnp.float32), 'wk': jax.random.normal(ks[2], (C, C), jnp.float32) * s, 'bk': jnp.zeros((C,), jnp.float32), 'wv': jax.random.normal(ks[3], (C, C), jnp.float32) * s, 'bv': jnp.zeros((C,), jnp.float32), 'wo': jax.random.normal(ks[4], (C, C), jnp.float32) * s, 'bo': jnp.zeros((C,), jnp.float32)}
    _L1_conv_all = _L1_conv_setup()
    _L1_conv_in = {k: v for k, v in _L1_conv_all.items() if k in ('gn_scale', 'gn_bias', 'wq', 'bq', 'wk', 'bk', 'wv', 'bv', 'wo', 'bo')}
    del _L1_conv_all

    def _L2_conv_setup():
        import jax, jax.numpy as jnp
        import numpy as np
        B, C, SIZE = (2, 256, 48)
        HEADS, DHEAD = (8, 32)
        INNER = HEADS * DHEAD
        EPS = 1e-05

        def _ln(x, g, b):
            m = jnp.mean(x, axis=-1, keepdims=True)
            v = jnp.mean(jnp.square(x - m), axis=-1, keepdims=True)
            return (x - m) * jax.lax.rsqrt(v + EPS) * g + b
        key = jax.random.key(seed)
        ks = jax.random.split(key, 16)
        s = 0.02
        return {'x': jax.random.normal(ks[0], (B, C, SIZE, SIZE), dtype=jnp.float32), 'ln1_g': jnp.ones((C,), jnp.float32), 'ln1_b': jnp.zeros((C,), jnp.float32), 'wq': jax.random.normal(ks[1], (C, INNER), jnp.float32) * s, 'wkv': jax.random.normal(ks[2], (C, 2 * DHEAD), jnp.float32) * s, 'wo': jax.random.normal(ks[3], (INNER, C), jnp.float32) * s, 'ln2_g': jnp.ones((C,), jnp.float32), 'ln2_b': jnp.zeros((C,), jnp.float32), 'ff_ln1_g': jnp.ones((C,), jnp.float32), 'ff_ln1_b': jnp.zeros((C,), jnp.float32), 'ff_w1': jax.random.normal(ks[4], (C, C), jnp.float32) * s, 'ff_b1': jnp.zeros((C,), jnp.float32), 'ff_ln2_g': jnp.ones((C,), jnp.float32), 'ff_ln2_b': jnp.zeros((C,), jnp.float32), 'ff_w2': jax.random.normal(ks[5], (C, C), jnp.float32) * s, 'ff_b2': jnp.zeros((C,), jnp.float32)}
    _L2_conv_all = _L2_conv_setup()
    _L2_conv_in = {k: v for k, v in _L2_conv_all.items() if k in ('ln1_g', 'ln1_b', 'wq', 'wkv', 'wo', 'ln2_g', 'ln2_b', 'ff_ln1_g', 'ff_ln1_b', 'ff_w1', 'ff_b1', 'ff_ln2_g', 'ff_ln2_b', 'ff_w2', 'ff_b2')}
    del _L2_conv_all

    def _L3_conv_setup():
        import jax, jax.numpy as jnp
        import numpy as np
        NUM_GROUPS = 32
        EPS = 1e-06

        def group_norm(x, g, b):
            B, C, H, W = x.shape
            xr = x.reshape(B, NUM_GROUPS, C // NUM_GROUPS, H, W)
            mean = xr.mean(axis=(2, 3, 4), keepdims=True)
            var = xr.var(axis=(2, 3, 4), keepdims=True)
            xn = ((xr - mean) * jax.lax.rsqrt(var + EPS)).reshape(B, C, H, W)
            return xn * g[None, :, None, None] + b[None, :, None, None]
        key = jax.random.key(seed)
        ks = jax.random.split(key, 8)
        B, C, H, W = (4, 256, 32, 32)
        s = 1.0 / np.sqrt(C)
        return {'x': jax.random.normal(ks[0], (B, C, H, W), jnp.float32), 'norm_g': jnp.ones((C,), jnp.float32), 'norm_b': jnp.zeros((C,), jnp.float32), 'wq': jax.random.normal(ks[1], (C, C), jnp.float32) * s, 'bq': jnp.zeros((C,), jnp.float32), 'wk': jax.random.normal(ks[2], (C, C), jnp.float32) * s, 'bk': jnp.zeros((C,), jnp.float32), 'wv': jax.random.normal(ks[3], (C, C), jnp.float32) * s, 'bv': jnp.zeros((C,), jnp.float32), 'wo': jax.random.normal(ks[4], (C, C), jnp.float32) * s, 'bo': jnp.zeros((C,), jnp.float32)}
    _L3_conv_all = _L3_conv_setup()
    _L3_conv_in = {k: v for k, v in _L3_conv_all.items() if k in ('norm_g', 'norm_b', 'wq', 'bq', 'wk', 'bk', 'wv', 'bv', 'wo', 'bo')}
    del _L3_conv_all
    return {'x': x, 'L0_conv_Wq': _L0_conv_in['Wq'], 'L0_conv_bq': _L0_conv_in['bq'], 'L0_conv_Wk': _L0_conv_in['Wk'], 'L0_conv_bk': _L0_conv_in['bk'], 'L0_conv_Wv': _L0_conv_in['Wv'], 'L0_conv_bv': _L0_conv_in['bv'], 'L0_conv_gamma': _L0_conv_in['gamma'], 'L1_conv_gn_scale': _L1_conv_in['gn_scale'], 'L1_conv_gn_bias': _L1_conv_in['gn_bias'], 'L1_conv_wq': _L1_conv_in['wq'], 'L1_conv_bq': _L1_conv_in['bq'], 'L1_conv_wk': _L1_conv_in['wk'], 'L1_conv_bk': _L1_conv_in['bk'], 'L1_conv_wv': _L1_conv_in['wv'], 'L1_conv_bv': _L1_conv_in['bv'], 'L1_conv_wo': _L1_conv_in['wo'], 'L1_conv_bo': _L1_conv_in['bo'], 'L2_conv_ln1_g': _L2_conv_in['ln1_g'], 'L2_conv_ln1_b': _L2_conv_in['ln1_b'], 'L2_conv_wq': _L2_conv_in['wq'], 'L2_conv_wkv': _L2_conv_in['wkv'], 'L2_conv_wo': _L2_conv_in['wo'], 'L2_conv_ln2_g': _L2_conv_in['ln2_g'], 'L2_conv_ln2_b': _L2_conv_in['ln2_b'], 'L2_conv_ff_ln1_g': _L2_conv_in['ff_ln1_g'], 'L2_conv_ff_ln1_b': _L2_conv_in['ff_ln1_b'], 'L2_conv_ff_w1': _L2_conv_in['ff_w1'], 'L2_conv_ff_b1': _L2_conv_in['ff_b1'], 'L2_conv_ff_ln2_g': _L2_conv_in['ff_ln2_g'], 'L2_conv_ff_ln2_b': _L2_conv_in['ff_ln2_b'], 'L2_conv_ff_w2': _L2_conv_in['ff_w2'], 'L2_conv_ff_b2': _L2_conv_in['ff_b2'], 'L3_conv_norm_g': _L3_conv_in['norm_g'], 'L3_conv_norm_b': _L3_conv_in['norm_b'], 'L3_conv_wq': _L3_conv_in['wq'], 'L3_conv_bq': _L3_conv_in['bq'], 'L3_conv_wk': _L3_conv_in['wk'], 'L3_conv_bk': _L3_conv_in['bk'], 'L3_conv_wv': _L3_conv_in['wv'], 'L3_conv_bv': _L3_conv_in['bv'], 'L3_conv_wo': _L3_conv_in['wo'], 'L3_conv_bo': _L3_conv_in['bo']}

def reference(x, L0_conv_Wq, L0_conv_bq, L0_conv_Wk, L0_conv_bk, L0_conv_Wv, L0_conv_bv, L0_conv_gamma, L1_conv_gn_scale, L1_conv_gn_bias, L1_conv_wq, L1_conv_bq, L1_conv_wk, L1_conv_bk, L1_conv_wv, L1_conv_bv, L1_conv_wo, L1_conv_bo, L2_conv_ln1_g, L2_conv_ln1_b, L2_conv_wq, L2_conv_wkv, L2_conv_wo, L2_conv_ln2_g, L2_conv_ln2_b, L2_conv_ff_ln1_g, L2_conv_ff_ln1_b, L2_conv_ff_w1, L2_conv_ff_b1, L2_conv_ff_ln2_g, L2_conv_ff_ln2_b, L2_conv_ff_w2, L2_conv_ff_b2, L3_conv_norm_g, L3_conv_norm_b, L3_conv_wq, L3_conv_bq, L3_conv_wk, L3_conv_bk, L3_conv_wv, L3_conv_bv, L3_conv_wo, L3_conv_bo):
    import jax
    import jax.numpy as jnp

    def _L0_conv_ref(x, Wq, bq, Wk, bk, Wv, bv, gamma):
        import jax, jax.numpy as jnp
        import numpy as np
        C_IN = 256
        MID = C_IN // 8
        B, H, W = (4, 32, 32)
        b, c, h, w = x.shape
        n = h * w
        xf = x.reshape(b, c, n)
        Q = jnp.einsum('mc,bcn->bnm', Wq, xf) + bq
        K = jnp.einsum('mc,bcn->bmn', Wk, xf) + bk[None, :, None]
        V = jnp.einsum('oc,bcn->bon', Wv, xf) + bv[None, :, None]
        attn = jax.nn.softmax(jnp.einsum('bnm,bmj->bnj', Q, K), axis=-1)
        out = jnp.einsum('bcj,bij->bci', V, attn).reshape(b, c, h, w)
        return gamma[0] * out + x

    def _L1_conv_ref(x, gn_scale, gn_bias, wq, bq, wk, bk, wv, bv, wo, bo):
        import jax, jax.numpy as jnp
        import numpy as np
        NUM_GROUPS = 32
        EPS = 1e-06

        def group_norm(x, scale, bias):
            b, c, h, w = x.shape
            g = NUM_GROUPS
            xg = x.reshape(b, g, c // g, h, w)
            mean = xg.mean(axis=(2, 3, 4), keepdims=True)
            var = xg.var(axis=(2, 3, 4), keepdims=True)
            xg = (xg - mean) * jax.lax.rsqrt(var + EPS)
            x = xg.reshape(b, c, h, w)
            return x * scale[None, :, None, None] + bias[None, :, None, None]

        def conv1x1(x, w, b):
            return jnp.einsum('oc,bchw->bohw', w, x) + b[None, :, None, None]
        b, c, h, w = x.shape
        h_ = group_norm(x, gn_scale, gn_bias)
        q = conv1x1(h_, wq, bq).reshape(b, c, h * w)
        k = conv1x1(h_, wk, bk).reshape(b, c, h * w)
        v = conv1x1(h_, wv, bv).reshape(b, c, h * w)
        scale = c ** (-0.5)
        scores = jnp.einsum('bci,bcj->bij', q, k) * scale
        attn = jax.nn.softmax(scores, axis=2)
        out = jnp.einsum('bcj,bij->bci', v, attn).reshape(b, c, h, w)
        out = conv1x1(out, wo, bo)
        return x + out

    def _L2_conv_ref(x, ln1_g, ln1_b, wq, wkv, wo, ln2_g, ln2_b, ff_ln1_g, ff_ln1_b, ff_w1, ff_b1, ff_ln2_g, ff_ln2_b, ff_w2, ff_b2):
        import jax, jax.numpy as jnp
        import numpy as np
        B, C, SIZE = (2, 256, 48)
        HEADS, DHEAD = (8, 32)
        INNER = HEADS * DHEAD
        EPS = 1e-05

        def _ln(x, g, b):
            m = jnp.mean(x, axis=-1, keepdims=True)
            v = jnp.mean(jnp.square(x - m), axis=-1, keepdims=True)
            return (x - m) * jax.lax.rsqrt(v + EPS) * g + b
        b, c, hh, ww = x.shape
        n = hh * ww
        xs = x.reshape(b, c, n).transpose(0, 2, 1)
        x_ln = _ln(xs, ln1_g, ln1_b)
        q = (x_ln @ wq).reshape(b, n, HEADS, DHEAD).transpose(0, 2, 1, 3)
        q = q * DHEAD ** (-0.5)
        kv = x_ln @ wkv
        k, v = (kv[..., :DHEAD], kv[..., DHEAD:])
        sim = jnp.einsum('bhid,bjd->bhij', q, k)
        neg = -jnp.finfo(sim.dtype).max
        causal = jnp.triu(jnp.ones((n, n), bool), 1)
        sim = jnp.where(causal, neg, sim)
        attn = jax.nn.softmax(sim, axis=-1)
        out = jnp.einsum('bhij,bjd->bhid', attn, v)
        out = out.transpose(0, 2, 1, 3).reshape(b, n, INNER) @ wo
        av = _ln(out + xs, ln2_g, ln2_b)
        ff = _ln(av, ff_ln1_g, ff_ln1_b) @ ff_w1 + ff_b1
        ff = _ln(ff, ff_ln2_g, ff_ln2_b)
        ff = jax.nn.gelu(ff, approximate=False) @ ff_w2 + ff_b2
        y = ff + av
        return y.transpose(0, 2, 1).reshape(b, c, hh, ww)

    def _L3_conv_ref(x, norm_g, norm_b, wq, bq, wk, bk, wv, bv, wo, bo):
        import jax, jax.numpy as jnp
        import numpy as np
        NUM_GROUPS = 32
        EPS = 1e-06

        def group_norm(x, g, b):
            B, C, H, W = x.shape
            xr = x.reshape(B, NUM_GROUPS, C // NUM_GROUPS, H, W)
            mean = xr.mean(axis=(2, 3, 4), keepdims=True)
            var = xr.var(axis=(2, 3, 4), keepdims=True)
            xn = ((xr - mean) * jax.lax.rsqrt(var + EPS)).reshape(B, C, H, W)
            return xn * g[None, :, None, None] + b[None, :, None, None]
        B, C, H, W = x.shape
        N = H * W
        hn = group_norm(x, norm_g, norm_b)
        t = hn.reshape(B, C, N).transpose(0, 2, 1)
        q = jnp.einsum('bnc,oc->bno', t, wq) + bq
        k = jnp.einsum('bnc,oc->bno', t, wk) + bk
        v = jnp.einsum('bnc,oc->bno', t, wv) + bv
        scale = C ** (-0.5)
        w = jnp.einsum('bic,bjc->bij', q, k) * scale
        w = jax.nn.softmax(w, axis=2)
        h = jnp.einsum('bij,bjc->bic', w, v)
        out = jnp.einsum('bnc,oc->bno', h, wo) + bo
        return x + out.transpose(0, 2, 1).reshape(B, C, H, W)

    def _gn(v, G=32, eps=1e-05):
        B_, C_, H_, W_ = v.shape
        g = v.reshape(B_, G, C_ // G, H_, W_)
        m = jnp.mean(g, axis=(2, 3, 4), keepdims=True)
        s = jnp.var(g, axis=(2, 3, 4), keepdims=True)
        return ((g - m) / jnp.sqrt(s + eps)).reshape(v.shape)

    def _ln_c(v, eps=1e-06):
        m = jnp.mean(v, axis=1, keepdims=True)
        s = jnp.var(v, axis=1, keepdims=True)
        return (v - m) / jnp.sqrt(s + eps)

    def _ln_t(v, eps=1e-05):
        m = jnp.mean(v, axis=-1, keepdims=True)
        s = jnp.var(v, axis=-1, keepdims=True)
        return (v - m) / jnp.sqrt(s + eps)

    def _to_tokens(v):
        B_, C_, H_, W_ = v.shape
        return v.reshape(B_, C_, H_ * W_).transpose(0, 2, 1)

    def _from_tokens(t, like):
        B_, C_, H_, W_ = like.shape
        return t.transpose(0, 2, 1).reshape(B_, C_, H_, W_)
    x = _L0_conv_ref(x, L0_conv_Wq, L0_conv_bq, L0_conv_Wk, L0_conv_bk, L0_conv_Wv, L0_conv_bv, L0_conv_gamma)
    x = _L1_conv_ref(x, L1_conv_gn_scale, L1_conv_gn_bias, L1_conv_wq, L1_conv_bq, L1_conv_wk, L1_conv_bk, L1_conv_wv, L1_conv_bv, L1_conv_wo, L1_conv_bo)
    x = _L2_conv_ref(x, L2_conv_ln1_g, L2_conv_ln1_b, L2_conv_wq, L2_conv_wkv, L2_conv_wo, L2_conv_ln2_g, L2_conv_ln2_b, L2_conv_ff_ln1_g, L2_conv_ff_ln1_b, L2_conv_ff_w1, L2_conv_ff_b1, L2_conv_ff_ln2_g, L2_conv_ff_ln2_b, L2_conv_ff_w2, L2_conv_ff_b2)
    x = _L3_conv_ref(x, L3_conv_norm_g, L3_conv_norm_b, L3_conv_wq, L3_conv_bq, L3_conv_wk, L3_conv_bk, L3_conv_wv, L3_conv_bv, L3_conv_wo, L3_conv_bo)
    return x

_drawn_inputs = setup_inputs


def setup_inputs(seed=0):
    import zlib

    import numpy as np

    out = dict(_drawn_inputs(seed))
    spreads = {'L0_conv_bq': (0.0, 0.8),
     'L0_conv_bk': (0.0, 0.8),
     'L0_conv_bv': (0.0, 0.1),
     'L1_conv_gn_scale': (1.0, 0.2),
     'L1_conv_gn_bias': (0.0, 0.1),
     'L1_conv_bq': (0.0, 0.639),
     'L1_conv_bk': (0.0, 0.8),
     'L1_conv_bv': (0.0, 0.1),
     'L1_conv_bo': (0.0, 0.1),
     'L2_conv_ln1_g': (1.0, 0.6),
     'L2_conv_ln1_b': (0.0, 0.595),
     'L2_conv_ln2_g': (1.0, 0.2),
     'L2_conv_ln2_b': (0.0, 0.1),
     'L2_conv_ff_ln1_g': (1.0, 0.2),
     'L2_conv_ff_ln1_b': (0.0, 0.393),
     'L2_conv_ff_b1': (0.0, 0.1),
     'L2_conv_ff_ln2_g': (1.0, 0.2),
     'L2_conv_ff_ln2_b': (0.0, 0.321),
     'L2_conv_ff_b2': (0.0, 0.1),
     'L3_conv_norm_g': (1.0, 0.2),
     'L3_conv_norm_b': (0.0, 0.1),
     'L3_conv_bq': (0.0, 0.8),
     'L3_conv_bk': (0.0, 0.8),
     'L3_conv_bv': (0.0, 0.1),
     'L3_conv_bo': (0.0, 0.1)}
    factors = {'L0_conv_Wq': 4.66, 'L0_conv_Wk': 3.924, 'L2_conv_wq': 8.0}
    for name, (base, spread) in spreads.items():
        noise = np.random.default_rng([zlib.crc32(name.encode()), seed]).standard_normal(out[name].shape)
        drawn = base * np.exp(spread * noise) if base else spread * noise
        out[name] = jnp.asarray(drawn.astype(out[name].dtype))
    for name, factor in factors.items():
        out[name] = (out[name] * factor).astype(out[name].dtype)
    return out
```

```python
from contextlib import ExitStack

import concourse.bass as bass
from concourse import mybir

F32 = mybir.dt.float32
ALU = mybir.AluOpType
ACT = mybir.ActivationFunctionType
AX_X = mybir.AxisListType.X

P = 128
B, C, N = 4, 256, 1024
CT = C // P
NT = N // P
HALF = 512
NB = N // HALF
TPH = HALF // P
HEADS, DH = 8, 32
HG = 2
EPS_GN, EPS_LN = 1e-6, 1e-5
SLOTS = 3

VECS = ["L0_bv", "L1_g", "L1_b", "L1_bq", "L1_bk", "L1_bv", "L1_bo", "L2_ln1_g", "L2_ln1_b",
        "L2_f1_g", "L2_f1_b", "L2_f2_g", "L2_f2_b", "L2_b2", "L3_g", "L3_b", "L3_bq", "L3_bk",
        "L3_bv", "L3_bo"]
ROWS = ["ln2_g", "ln2_b", "ff_b1"]

START = 1

DVE_STEPS = 94


def causal_blocks():
    return [(0, 0), (0, 1), (1, 1), (1, 0)]


def causal_schedule():
    blocks = causal_blocks()

    def max_events(k):
        hg, ib = blocks[k]
        out = []
        for t in range(TPH * ib, TPH * (ib + 1)):
            end = (t + 1) * P
            for ch, (lo, hi) in enumerate([(0, end)] if end <= HALF else [(0, HALF), (HALF, end)]):
                out.append([("max", k, t, ch, lo, hi, pair) for pair in range(2)])
        return out

    events = [e for two in max_events(0) for e in two] + [("shift", 0)]
    pending = None
    step = 0
    for k, (hg, ib) in enumerate(blocks):
        ahead = max_events(k + 1) if k + 1 < len(blocks) else []
        tiles = TPH * (ib + 1)
        done = 0
        for jt in range(tiles):
            events += [("exp", k, jt, pair, step) for pair in range(2)]
            if pending:
                events.append(pending)
            pending = ("values", k, jt, step)
            step += 1
            upto = len(ahead) * (jt + 1) // tiles
            events += [e for two in ahead[done:upto] for e in two]
            done = upto
        if ahead:
            events.append(("shift", k + 1))
    return events + [pending]


def attention_units(layer):
    out = [(f"{layer}.s0", "act"), (f"{layer}.s1", "act")]
    for t in range(NT):
        out.append((f"{layer}.t{t}", "act"))
        if t + 2 < NT:
            out.append((f"{layer}.s{t + 2}", "act"))
    return out


def event_name(e):
    return "L2." + ".".join(map(str, e[:3] if e[0] == "values" else e[:4] + e[-1:]))


def ring_units():
    units = [("L0.q", "act"), ("L0.k", "dve"), ("L0.v0", "dve"), ("L0.v1", "act")]
    units += attention_units("L0")
    for layer in ("L1", "L3"):
        if layer == "L3":
            units += [("L2.xt0", "act"), ("L2.xt1", "act"), ("L2.xn0", "act"), ("L2.xn1", "act"),
                      ("L2.k", "dve"), ("L2.q0", "act"), ("L2.vt", "dve"), ("L2.q1", "act"),
                      ("L2.v", "dve")]
            for e in causal_schedule():
                if e[0] != "values":
                    units.append((event_name(e), "dve" if e[0] == "max" else "act"))
            units += [("L2.wo1", "dve"), ("L2.wo0", "dve"), ("L2.ta1", "act"), ("L2.w1_1", "dve"),
                      ("L2.ta0", "act"), ("L2.w1_0", "dve"), ("L2.tg1", "act"), ("L2.w2_1", "act"),
                      ("L2.tg0", "act"), ("L2.w2_0", "act")]
        units += [(f"{layer}.gn", "dve"), (f"{layer}.q0", "act"), (f"{layer}.k0", "dve"),
                  (f"{layer}.q1", "act"), (f"{layer}.k1", "dve"), (f"{layer}.v0", "dve"),
                  (f"{layer}.v1", "act")]
        units += attention_units(layer)
    return units


def accumulator_uses():
    full = [(ib, ct) for ib in range(NB) for ct in range(CT)]
    return ([(f"L0.{ib}{ct}", (ct,)) for ib, ct in full] + [(f"L1.{ib}{ct}", (ct,)) for ib, ct in full]
            + [(f"L2.{k}", (0, 1)) for k in range(len(causal_blocks()))]
            + [(f"L3.{ib}{ct}", (ct,)) for ib, ct in full])


def build(nc, t):
    units = ring_units()
    number = {name: u for u, (name, _) in enumerate(units)}
    reader = dict(units)
    U = len(units)
    rank, total = {}, {"act": 0, "dve": 0}
    for name, eng in units:
        total[eng] += 1
        rank[name] = total[eng]
    acc_uses = accumulator_uses()
    acc_no = {name: i for i, (name, _) in enumerate(acc_uses)}
    ACCS = len(acc_uses)
    schedule = causal_schedule()
    blocks = causal_blocks()
    norms = ["L1.gn", "L2.ln1.0", "L2.ln1.1", "L2.ln2.1", "L2.f1.1", "L2.ln2.0", "L2.f1.0",
             "L2.f2.1", "L2.f2.0", "L3.gn"]
    norm_no = {name: i for i, name in enumerate(norms)}
    NORMS = len(norms)
    diagonal = [e for e in schedule if e[0] == "exp" and e[2] >= TPH * blocks[e[1]][1]]
    DIAG = len(diagonal)
    last_max = {e[1]: event_name(e) for e in schedule if e[0] == "max"}
    LATE = sum(ib for _, ib in blocks)
    diag_no = {event_name(e): i for i, e in enumerate(diagonal)}

    with ExitStack() as ctx:
        def sb(name, shape):
            return ctx.enter_context(nc.sbuf_tensor(name, shape, F32))

        def sem(name):
            return ctx.enter_context(nc.semaphore(name))

        wqk0 = sb("wqk0", [P, 2, CT, 4, DH])
        bqk0 = sb("bqk0", [P, 2])
        wv0 = sb("wv0", [P, CT, C])
        gamma = sb("gamma", [P, 1])
        vecs = sb("vecs", [P, len(VECS), CT])
        rows = sb("rows", [P, len(ROWS), C])
        consts = sb("consts", [P, 3, P])
        wq, wk, wv, woT, wvo, bqs, bvo = {}, {}, {}, {}, {}, {}, {}
        for l in ("L1", "L3"):
            wq[l], wk[l] = sb(f"{l}_wq", [P, CT, C]), sb(f"{l}_wk", [P, CT, C])
            wv[l], woT[l] = sb(f"{l}_wv", [P, CT, C]), sb(f"{l}_woT", [P, CT, C])
            wvo[l] = sb(f"{l}_wvo", [P, CT, C])
            bqs[l] = sb(f"{l}_bqs", [P, CT])
            bvo[l] = sb(f"{l}_bvo", [P, CT])
        wq2 = sb("wq2", [P, CT, C])
        wk2 = sb("wk2", [P, CT, 4, DH])
        wv2 = sb("wv2", [P, CT, DH])
        wo2, ffw1, ffw2 = sb("wo2", [P, HG, C]), sb("ffw1", [P, CT, C]), sb("ffw2", [P, CT, C])
        ones = sb("ones", [P, P])
        idle_act = sb("idle_act", [P, 1])
        idle_pool, idle_dve = sb("idle_pool", [P, DIAG]), sb("idle_dve", [P, NORMS])
        half_neg = sb("half_neg", [P, 4])
        ident, group_mean, causal = consts[:, 0, :], consts[:, 1, :], consts[:, 2, :]

        xin = sb("xin", [P, CT, N])
        x = sb("x", [P, CT, N])
        y = sb("y", [P, CT, N])
        h = sb("h", [P, CT, N])
        q, k = sb("q", [P, CT, N]), sb("k", [P, CT, N])
        vt = sb("vt", [P, NT, C])
        probs = sb("probs", [P, SLOTS, N])
        probsT = sb("probsT", [P, NB, NT, HALF])
        heads_p = probsT.ap() if hasattr(probsT, "ap") else probsT
        neg_max, row_sum, row_inv = sb("neg_max", [P, NT]), sb("row_sum", [P, NT]), sb("row_inv", [P, NT])
        gn_stats = sb("gn_stats", [P, CT, NB, 6])
        gn_mv, gn_in, gn_out = sb("gn_mv", [P, CT, 2]), sb("gn_in", [P, CT, 2]), sb("gn_out", [P, CT, 2])
        gn_sq, gn_sc, gn_msc, gn_nb = (sb(f"gn_{s}", [P, CT]) for s in ("sq", "sc", "msc", "nb"))
        var_eps, rstd = sb("var_eps", [P, NORMS, 4]), sb("rstd", [P, NORMS, 4])
        xs, av, an = sb("xs", [P, NT, C]), sb("av", [P, NT, C]), sb("an", [P, NT, C])
        ln_stats, ln_mv = sb("ln_stats", [P, NORMS, TPH, 6]), sb("ln_mv", [P, NORMS, TPH, 2])
        vT2, v2 = sb("vT2", [P, HALF]), sb("v2", [P, NT, DH])
        part_max = sb("part_max", [P, TPH, 2, 4])
        max_cols = sb("max_cols", [P, 2, TPH, P])
        max_rows = sb("max_rows", [P, 2, HALF])
        inv_den = sb("inv_den", [P, HALF])
        heads_out = sb("heads_out", [P, HG, N])

        def causal_probs(step, pair, n):
            flat = probsT[:, :, :, :].rearrange("p a b n -> p (a b) n")
            s = (step % 4) * 4 + 2 * pair
            return flat[:, s:s + 2, 0:n]

        ring = ctx.enter_context(nc.psum_tensor("ring", [P, SLOTS, 2, HALF], F32))
        acc = ctx.enter_context(nc.psum_tensor("acc", [P, 2, HALF], F32))

        weights_in = sem("weights_in")
        x_in = sem("x_in")
        y_out = sem("y_out")
        y_free = sem("y_free")
        ring_filled = sem("ring_filled")
        act_read = sem("act_read")
        dve_read = sem("dve_read")
        acc_filled = sem("acc_filled")
        acc_read = sem("acc_read")
        row_max_ready = sem("row_max_ready")
        probs_scaled = sem("probs_scaled")
        gn_in_ready = sem("gn_in_ready")
        gn_coef_ready = sem("gn_coef_ready")
        h_dve, h_act = sem("h_dve"), sem("h_act")
        var_ready = sem("var_ready")
        rstd_ready = sem("rstd_ready")
        ln_ready = sem("ln_ready")
        max_ready = sem("max_ready")
        diag_masked = sem("diag_masked")
        dve_step = sem("dve_step")
        prep_mm, prep_done, setup = sem("prep_mm"), sem("prep_done"), sem("setup")

        unit_slot = {name: number[name] % SLOTS for name in number}

        def slot(name):
            return ring[:, unit_slot[name], :, :]

        def wait_read(eng, b, name):
            e = reader[name]
            eng.wait_ge(act_read if e == "act" else dve_read, b * total[e] + START + rank[name])

        def wait_filled(eng, b, name):
            eng.wait_ge(ring_filled, b * U + (number[name] + 1))

        def wait_acc_read(eng, b, name):
            eng.wait_ge(acc_read, b * ACCS + START + (acc_no[name] + 1))

        def vec(name, ct):
            return vecs[:, VECS.index(name), ct:ct + 1]

        LOADS = [
            (wv0[:, :, :], t["L0_WvT"].rearrange("(c p) o -> p c o", p=P)),
            (vecs[:, :, :], t["vecs"]),
            (consts[:, :, :], t["consts"]),
            (gamma[:, :], t["gamma"].partition_broadcast(P)),
            (wq2[:, :, :], t["L2_wq"].rearrange("(c p) o -> p c o", p=P)),
            (wv2[:, :, :], t["L2_wkv"][:, DH:2 * DH].rearrange("(c p) o -> p c o", p=P)),
            (wo2[:, :, :], t["L2_wo"].rearrange("(c p) o -> p c o", p=P)),
            (ffw1[:, :, :], t["L2_w1"].rearrange("(c p) o -> p c o", p=P)),
            (ffw2[:, :, :], t["L2_w2"].rearrange("(c p) o -> p c o", p=P)),
        ]
        for g in range(4):
            for i, w in enumerate(("L0_WqT", "L0_WkT")):
                LOADS.append((wqk0[:, i, :, g, :], t[w].rearrange("(c p) m -> p c m", p=P)))
                LOADS.append((bqk0[DH * g:DH * (g + 1), i:i + 1], t[("L0_bq", "L0_bk")[i]]))
            LOADS.append((wk2[:, :, g, :], t["L2_wkv"][:, 0:DH].rearrange("(c p) o -> p c o", p=P)))
        for i in range(len(ROWS)):
            LOADS.append((rows[:, i, :], t["rows"][i, :].partition_broadcast(P)))
        for l in ("L1", "L3"):
            for w, name in ((wq[l], "wqT"), (wk[l], "wkT"), (wv[l], "wv"), (woT[l], "woT")):
                LOADS.append((w[:, :, :], t[f"{l}_{name}"].rearrange("(c p) o -> p c o", p=P)))
        ALL_LOADED = 16 * len(LOADS)

        block = ctx.enter_context(nc.Block())

        @block.sync
        def _(sp):
            x_dram = t["x"].rearrange("b (c p) h w -> b p c (h w)", p=P)
            y_dram = t["out"].rearrange("b (c p) h w -> b p c (h w)", p=P)
            sp.dma_start(xin[:, :, :], x_dram[0]).then_inc(x_in, 16)
            for dst, src in LOADS:
                sp.dma_start(dst, src).then_inc(weights_in, 16)

            sp.sem_inc(y_free, 1)

            def store(b):
                for ib in range(NB):
                    wait_acc_read(sp, b, f"L3.{ib}{CT - 1}")
                    sl = slice(ib * HALF, (ib + 1) * HALF)
                    sp.dma_start(y_dram[b][:, :, sl], y[:, :, sl]).then_inc(y_out, 16)
                sp.wait_ge(y_out, b * (16 * NB) + 16 * NB)
                sp.sem_inc(y_free, 1)

            with sp.Fori(0, B - 1) as b:
                wait_acc_read(sp, b, f"L0.{NB - 1}{CT - 1}")
                sp.dma_start(xin[:, :, :], x_dram[b + 1]).then_inc(x_in, 16)
                store(b)
            store(B - 1)

        @block.gpsimd
        def _(pool):
            pool.memset(ones[:, :], 1.0).then_inc(setup, 1)
            pool.memset(half_neg[:, :], -0.5).then_inc(setup, 1)
            pool.memset(max_cols[:, :, :, :], 0.0).then_inc(setup, 1)
            pool.memset(vT2[:, :], 0.0).then_inc(setup, 1)
            pool.wait_ge(setup, 4)

            def root(b, name):
                n = norm_no[name]
                w = CT if name.endswith("gn") else TPH
                pool.wait_ge(var_ready, b * NORMS + (n + 1))
                pool.tensor_tensor(rstd[:, n, 0:w], var_eps[:, n, 0:w], half_neg[:, 0:w],
                                   ALU.pow).then_inc(rstd_ready, 1)

            with pool.Fori(0, B) as b:
                for name in norms[:3]:
                    root(b, name)
                for i, e in enumerate(diagonal):
                    _, kk, jt, pair, step = e
                    wait_read(pool, b, event_name(e))
                    d = causal_probs(step, pair, P)
                    pool.tensor_tensor(idle_pool[:, i:i + 1], half_neg[:, 0:1], half_neg[:, 0:1], ALU.mult)
                    pool.affine_select(out=d, in_=d, pattern=[[0, 2], [1, P]], compare_op=ALU.is_ge,
                                       fill=0.0, base=0, channel_multiplier=-1).then_inc(diag_masked, 1)
                for name in norms[3:]:
                    root(b, name)

        @block.tensor
        def _(pe):
            mm = nc.tensor.matmul

            def open_unit(b, name):
                u = number[name]
                if u >= SLOTS:
                    wait_read(pe, b, units[u - SLOTS][0])
                else:
                    pe.wait_ge(act_read, b * total["act"] + START)
                    pe.wait_ge(dve_read, b * total["dve"] + START)
                return slot(name)

            def open_acc(b, name):
                i = acc_no[name]
                before = [j for j in range(i) if set(acc_uses[j][1]) & set(acc_uses[i][1])]
                pe.wait_ge(acc_read, b * ACCS + START + (before[-1] + 1 if before else 0))

            pe.wait_ge(weights_in, ALL_LOADED)
            for l, out in (("L1", acc), ("L3", ring[:, 0, :, :])):
                for ci in range(CT):
                    for m in range(CT):
                        mm(out[:, ci, 0:C], wv[l][:, m, ci * P:(ci + 1) * P], woT[l][:, m, :],
                           start=m == 0, stop=m == CT - 1)
                for co in range(CT):
                    for m in range(CT):
                        last = mm(out[:, co, C:C + 1], woT[l][:, m, co * P:(co + 1) * P],
                                  vec(f"{l}_bv", m), start=m == 0, stop=m == CT - 1)
                last.then_inc(prep_mm, 1)
            pe.wait_ge(prep_done, 1)
            pe.wait_ge(setup, 4)

            def project(b, name, w, src, cols):
                o = open_unit(b, name)
                for hf in range(NB):
                    for c in range(CT):
                        last = mm(o[:, hf, :], w(c), src[:, c, hf * HALF:(hf + 1) * HALF],
                                  start=c == 0, stop=c == CT - 1)
                last.then_inc(ring_filled, 1)

            def token_project(b, name, src, w, t0):
                o = open_unit(b, name).rearrange("p b (s c) -> p (b s) c", c=C)
                for i in range(TPH):
                    for c in range(CT):
                        last = mm(o[:, i, :], src[:, c, (t0 + i) * P:(t0 + i + 1) * P], w[:, c, :],
                                  start=c == 0, stop=c == CT - 1)
                last.then_inc(ring_filled, 1)

            def full_attention(b, l):
                def scores(ti):
                    o = open_unit(b, f"{l}.s{ti}")
                    for hf in range(NB):
                        ks = slice(hf * HALF, (hf + 1) * HALF)
                        if l == "L0":
                            r = DH * ((2 * ti + hf) % 4)
                            last = mm(o[:, hf, :], q[r:r + DH, 0, ti * P:(ti + 1) * P],
                                      k[r:r + DH, 0, ks], start=True, stop=True)
                        else:
                            for c in range(CT):
                                last = mm(o[:, hf, :], q[:, c, ti * P:(ti + 1) * P], k[:, c, ks],
                                          start=c == 0, stop=c == CT - 1)
                    last.then_inc(ring_filled, 1)

                def turn(ti):
                    o = open_unit(b, f"{l}.t{ti}").rearrange("p b (s n) -> p (b s) n", n=P)
                    pe.wait_ge(probs_scaled, b * (3 * NT) + ("L0", "L1", "L3").index(l) * NT + ti + 1)
                    for j in range(NT):
                        last = nc.tensor.transpose(o[:, j, :], probs[:, ti % SLOTS, j * P:(j + 1) * P], ident)
                    last.then_inc(ring_filled, 1)

                def values(ib, part):
                    ct, j0 = divmod(part * TPH, NT)
                    if j0 == 0:
                        open_acc(b, f"{l}.{ib}{ct}")
                    for j in range(j0, j0 + TPH):
                        last = mm(acc[:, ct, :], vt[:, j, ct * P:(ct + 1) * P], probsT[:, ib, j, :],
                                  start=j == 0, stop=j == NT - 1)
                    if j0 + TPH == NT:
                        last.then_inc(acc_filled, 1)

                scores(0)
                scores(1)
                for ti in range(NT):
                    turn(ti)
                    if ti + 2 < NT:
                        scores(ti + 2)
                    if ti == TPH:
                        wait_read(pe, b, f"{l}.v1")
                    if ti >= TPH:
                        values(0, ti - TPH)
                wait_read(pe, b, f"{l}.t{NT - 1}")
                for part in range(TPH):
                    values(1, part)

            def group_normed(b, l):
                pe.wait_ge(gn_in_ready, b * 2 + (1 if l == "L1" else 2))
                o = open_unit(b, f"{l}.gn")
                mm(o[:, 0, 0:2 * CT], group_mean, gn_in[:, :, :].rearrange("p c s -> p (c s)"),
                   start=True, stop=True).then_inc(ring_filled, 1)
                pe.wait_ge(h_dve, b * 2 + (1 if l == "L1" else 2))
                pe.wait_ge(h_act, b * 2 + (1 if l == "L1" else 2))
                for m in range(CT):
                    project(b, f"{l}.q{m}", lambda c: wq[l][:, c, m * P:(m + 1) * P], h, None)
                    project(b, f"{l}.k{m}", lambda c: wk[l][:, c, m * P:(m + 1) * P], h, None)
                for i in range(2):
                    token_project(b, f"{l}.v{i}", h, wvo[l], i * TPH)
                wait_read(pe, b, f"{l}.q1")
                wait_read(pe, b, f"{l}.k1")
                full_attention(b, l)

            def causal_layer(b):
                for hf in range(NB):
                    wait_acc_read(pe, b, f"L1.{hf}{CT - 1}")
                    o = open_unit(b, f"L2.xt{hf}").rearrange("p b (s c n) -> p (b s) c n", c=CT, n=P)
                    for i in range(TPH):
                        ti = hf * TPH + i
                        for c in range(CT):
                            last = nc.tensor.transpose(o[:, i, c, :], x[:, c, ti * P:(ti + 1) * P], ident)
                    last.then_inc(ring_filled, 1)

                def turn_normed(name, hf, nth):
                    pe.wait_ge(ln_ready, b * 6 + nth)
                    o = open_unit(b, name)
                    for i in range(TPH):
                        for c in range(CT):
                            last = nc.tensor.transpose(o[:, c, i * P:(i + 1) * P],
                                                       an[:, hf * TPH + i, c * P:(c + 1) * P], ident)
                    last.then_inc(ring_filled, 1)

                turn_normed("L2.xn0", 0, 1)
                turn_normed("L2.xn1", 1, 2)
                wait_read(pe, b, "L2.xn1")
                project(b, "L2.k", lambda c: wk2[:, c, :, :].rearrange("p g d -> p (g d)"), h, None)
                project(b, "L2.q0", lambda c: wq2[:, c, 0:P], h, None)
                o = open_unit(b, "L2.vt")
                for c in range(CT):
                    for hf in range(NB):
                        last = mm(o[hf * DH:(hf + 1) * DH, 0, :], wv2[:, c, :],
                                  h[:, c, hf * HALF:(hf + 1) * HALF], start=c == 0, stop=c == CT - 1)
                last.then_inc(ring_filled, 1)
                project(b, "L2.q1", lambda c: wq2[:, c, P:2 * P], h, None)
                wait_read(pe, b, "L2.vt")
                o = open_unit(b, "L2.v").rearrange("p b (s n) -> p (b s) n", n=P)
                for i in range(TPH):
                    last = nc.tensor.transpose(o[:, i, :], vT2[:, i * P:(i + 1) * P], ident)
                last.then_inc(ring_filled, 1)
                wait_read(pe, b, "L2.q1")
                wait_read(pe, b, "L2.v")

                for e in schedule:
                    kk = e[1]
                    hg, ib = blocks[kk]
                    if e[0] == "max":
                        _, _, ti, _, lo, hi, pair = e
                        o = open_unit(b, event_name(e))
                        for i in range(2):
                            r = DH * (2 * pair + i)
                            last = mm(o[:, i, 0:hi - lo], q[r:r + DH, hg, ti * P:(ti + 1) * P],
                                      k[r:r + DH, 0, lo:hi], start=True, stop=True)
                        last.then_inc(ring_filled, 1)
                    elif e[0] == "shift":
                        if ib == 0:
                            wait_read(pe, b, last_max[kk])
                        else:
                            pe.wait_ge(max_ready, b * LATE + sum(f for _, f in blocks[:kk + 1]))
                        o = open_unit(b, event_name(e))
                        for i in range(TPH):
                            last = nc.tensor.transpose(o[:, 0, i * P:(i + 1) * P], max_cols[:, kk % 2, i, :], ident)
                        last.then_inc(ring_filled, 1)
                    elif e[0] == "exp":
                        _, _, jt, pair, step = e
                        i0 = max(jt * P, ib * HALF)
                        n = (ib + 1) * HALF - i0
                        if jt == 0 and pair == 0:
                            wait_read(pe, b, event_name(("shift", kk)))
                        o = open_unit(b, event_name(e))
                        for i in range(2):
                            r = DH * (2 * pair + i)
                            mm(o[:, i, 0:n], k[r:r + DH, 0, jt * P:(jt + 1) * P], q[r:r + DH, hg, i0:i0 + n],
                               start=True, stop=False)
                        for i in range(2):
                            r = DH * (2 * pair + i)
                            last = mm(o[:, i, 0:n], ones[r:r + 1, :],
                                      max_rows[r:r + 1, kk % 2, HALF - n:HALF], start=False, stop=True)
                        last.then_inc(ring_filled, 1)
                    else:
                        _, _, jt, step = e
                        i0 = max(jt * P, ib * HALF)
                        n = (ib + 1) * HALF - i0
                        last_jt = TPH * (ib + 1) - 1
                        if jt == 0:
                            open_acc(b, f"L2.{kk}")
                        name = event_name(("exp", kk, jt, 1, step))
                        if name in diag_no:
                            pe.wait_ge(diag_masked, b * DIAG + diag_no[name] + 1)
                        else:
                            wait_read(pe, b, name)
                        for bank, w in ((0, v2[:, jt, :]), (1, ones[:, 0:DH])):
                            for a in range(4):
                                last = mm(acc[DH * a:DH * (a + 1), bank, HALF - n:HALF], w,
                                          causal_probs(step, a // 2, n)[:, a % 2, :],
                                          start=jt == 0, stop=jt == last_jt)
                        if jt == last_jt:
                            last.then_inc(acc_filled, 1)

                for hf in (1, 0):
                    wait_acc_read(pe, b, "L2.2" if hf else "L2.3")
                    token_project(b, f"L2.wo{hf}", heads_out, wo2, hf * TPH)
                for n, hf in enumerate((1, 0)):
                    turn_normed(f"L2.ta{hf}", hf, 3 + n)
                    wait_read(pe, b, f"L2.ta{hf}")
                    token_project(b, f"L2.w1_{hf}", h, ffw1, hf * TPH)
                for n, hf in enumerate((1, 0)):
                    turn_normed(f"L2.tg{hf}", hf, 5 + n)
                    wait_read(pe, b, f"L2.tg{hf}")
                    o = open_unit(b, f"L2.w2_{hf}")
                    for co in range(CT):
                        cs = slice(co * P, (co + 1) * P)
                        for c in range(CT):
                            mm(o[:, co, :], ffw2[:, c, cs], q[:, c, hf * HALF:(hf + 1) * HALF],
                               start=c == 0, stop=False)
                        for i in range(TPH):
                            last = mm(o[:, co, i * P:(i + 1) * P], av[:, hf * TPH + i, cs], ident,
                                      start=False, stop=i == TPH - 1)
                    last.then_inc(ring_filled, 1)

            with pe.Fori(0, B) as b:
                pe.wait_ge(x_in, b * 16 + 16)
                for i, name in enumerate(("L0.q", "L0.k")):
                    project(b, name, lambda c: wqk0[:, i, c, :, :].rearrange("p g d -> p (g d)"), xin, None)
                for i in range(2):
                    token_project(b, f"L0.v{i}", xin, wv0, i * TPH)
                wait_read(pe, b, "L0.q")
                wait_read(pe, b, "L0.k")
                full_attention(b, "L0")
                group_normed(b, "L1")
                causal_layer(b)
                group_normed(b, "L3")

        @block.scalar
        def _(act):
            act.wait_ge(weights_in, ALL_LOADED)
            act.wait_ge(prep_done, 1)
            nc.scalar.copy(idle_act[:, :], gamma[:, :]).then_inc(act_read, START)

            def flat(name):
                return slot(name).rearrange("p b n -> p (b n)")

            def full_attention(b, l):
                def exp(ti):
                    act.wait_ge(row_max_ready, b * (3 * NT) + ("L0", "L1", "L3").index(l) * NT + ti + 1)
                    if ti >= SLOTS:
                        wait_filled(act, b, f"{l}.t{ti - SLOTS}")
                    nc.scalar.activation(probs[:, ti % SLOTS, :], flat(f"{l}.s{ti}"), ACT.Exp,
                                         bias=neg_max[:, ti:ti + 1],
                                         accum_out=row_sum[:, ti:ti + 1]).then_inc(act_read, 1)

                def turned(ti):
                    wait_filled(act, b, f"{l}.t{ti}")
                    nc.scalar.copy(probsT[:, ti // TPH, :, (ti % TPH) * P:(ti % TPH + 1) * P],
                                   slot(f"{l}.t{ti}").rearrange("p b (s n) -> p (b s) n", n=P)
                                   ).then_inc(act_read, 1)

                exp(0)
                exp(1)
                for ti in range(NT):
                    turned(ti)
                    if ti + 2 < NT:
                        exp(ti + 2)

            def group_normed(b, l):
                n = 1 if l == "L1" else 2
                act.wait_ge(gn_coef_ready, b * 2 + n)
                nc.scalar.activation(h[:, 1, :], x[:, 1, :], ACT.Identity, scale=gn_sc[:, 1:2],
                                     bias=gn_nb[:, 1:2]).then_inc(h_act, 1)
                for m in range(CT):
                    wait_filled(act, b, f"{l}.q{m}")
                    nc.scalar.activation(q[:, m, :], flat(f"{l}.q{m}"), ACT.Identity, scale=C ** -0.5,
                                         bias=bqs[l][:, m:m + 1]).then_inc(act_read, 1)
                wait_filled(act, b, f"{l}.v1")
                nc.scalar.copy(vt[:, TPH:NT, :].rearrange("p t c -> p (t c)"), flat(f"{l}.v1")
                               ).then_inc(act_read, 1)
                full_attention(b, l)

            def causal_layer(b):
                for hf in range(NB):
                    wait_filled(act, b, f"L2.xt{hf}")
                    nc.scalar.copy(xs[:, hf * TPH:(hf + 1) * TPH, :].rearrange("p t c -> p (t c)"),
                                   flat(f"L2.xt{hf}")).then_inc(act_read, 1)

                def scaled(name, dst, hf, func, g, bias):
                    wait_filled(act, b, name)
                    for c in range(CT):
                        last = nc.scalar.activation(dst[:, c, hf * HALF:(hf + 1) * HALF], slot(name)[:, c, :],
                                                    func, scale=vec(g, c), bias=vec(bias, c))
                    last.then_inc(act_read, 1)

                for hf in range(NB):
                    scaled(f"L2.xn{hf}", h, hf, ACT.Identity, "L2_ln1_g", "L2_ln1_b")
                for m in range(HG):
                    wait_filled(act, b, f"L2.q{m}")
                    nc.scalar.activation(q[:, m, :], flat(f"L2.q{m}"), ACT.Copy,
                                         scale=DH ** -0.5).then_inc(act_read, 1)
                for e in schedule:
                    if e[0] == "shift":
                        wait_filled(act, b, event_name(e))
                        nc.scalar.copy(max_rows[:, e[1] % 2, :], slot(event_name(e))[:, 0, :]).then_inc(act_read, 1)
                    elif e[0] == "exp":
                        _, kk, jt, pair, step = e
                        ib = blocks[kk][1]
                        n = (ib + 1) * HALF - max(jt * P, ib * HALF)
                        wait_filled(act, b, event_name(e))
                        nc.scalar.activation(causal_probs(step, pair, n), slot(event_name(e))[:, :, 0:n],
                                             ACT.Exp).then_inc(act_read, 1)
                for hf in (1, 0):
                    scaled(f"L2.ta{hf}", h, hf, ACT.Identity, "L2_f1_g", "L2_f1_b")
                for hf in (1, 0):
                    scaled(f"L2.tg{hf}", q, hf, ACT.Gelu, "L2_f2_g", "L2_f2_b")
                    wait_filled(act, b, f"L2.w2_{hf}")
                    for c in range(CT):
                        last = nc.scalar.activation(x[:, c, hf * HALF:(hf + 1) * HALF],
                                                    slot(f"L2.w2_{hf}")[:, c, :], ACT.Identity,
                                                    bias=vec("L2_b2", c))
                    last.then_inc(act_read, 1)

            with act.Fori(0, B) as b:
                wait_filled(act, b, "L0.q")
                nc.scalar.activation(q[:, 0, :], flat("L0.q"), ACT.Identity, bias=bqk0[:, 0:1]).then_inc(act_read, 1)
                wait_filled(act, b, "L0.v1")
                nc.scalar.copy(vt[:, TPH:NT, :].rearrange("p t c -> p (t c)"), flat("L0.v1")).then_inc(act_read, 1)
                full_attention(b, "L0")
                group_normed(b, "L1")
                causal_layer(b)
                group_normed(b, "L3")

        @block.vector
        def _(dve):
            steps = [0]
            v = nc.vector

            def then(b, ins):
                steps[0] += 1
                ins.then_inc(dve_step, 1)
                dve.wait_ge(dve_step, b * DVE_STEPS + steps[0])

            def flat(name):
                return slot(name).rearrange("p b n -> p (b n)")

            dve.wait_ge(setup, 4)
            dve.wait_ge(weights_in, ALL_LOADED)
            for n, (l, o) in enumerate((("L1", acc), ("L3", ring[:, 0, :, :]))):
                dve.wait_ge(prep_mm, n + 1)
                v.tensor_copy(wvo[l][:, :, :], o[:, :, 0:C])
                v.tensor_tensor(bvo[l][:, :], o[:, :, C:C + 1].rearrange("p c o -> p (c o)"),
                                vecs[:, VECS.index(f"{l}_bo"), :], ALU.add)
                v.tensor_scalar(bqs[l][:, :], vecs[:, VECS.index(f"{l}_bq"), :], C ** -0.5, None, ALU.mult)
            v.tensor_scalar(wv0[:, :, :], wv0[:, :, :], gamma[:, 0:1], None, ALU.mult)
            bv0 = vecs[:, VECS.index("L0_bv"), :]
            v.tensor_scalar(bv0, bv0, gamma[:, 0:1], None, ALU.mult).then_inc(prep_done, 1)
            dve.wait_ge(prep_done, 1)
            v.memset(idle_dve[:, 0:1], 0.0).then_inc(dve_read, START)
            dve.wait_ge(dve_read, START)
            v.memset(idle_dve[:, 0:1], 0.0).then_inc(acc_read, START)
            dve.wait_ge(acc_read, START)

            def full_attention(b, l, base, bias, dst):
                first = b * (3 * NT) + ("L0", "L1", "L3").index(l) * NT

                def row_max(ti):
                    wait_filled(dve, b, f"{l}.s{ti}")
                    v.tensor_reduce(neg_max[:, ti:ti + 1], flat(f"{l}.s{ti}"), AX_X, ALU.max,
                                    negate=True).then_inc(row_max_ready, 1)

                def scale(ti):
                    wait_read(dve, b, f"{l}.s{ti}")
                    then(b, v.reciprocal(row_inv[:, ti:ti + 1], row_sum[:, ti:ti + 1]))
                    v.tensor_scalar(probs[:, ti % SLOTS, :], probs[:, ti % SLOTS, :], row_inv[:, ti:ti + 1],
                                    None, ALU.mult).then_inc(probs_scaled, 1)

                def residual(ib, ct):
                    sl = slice(ib * HALF, (ib + 1) * HALF)
                    dve.wait_ge(acc_filled, b * ACCS + acc_no[f"{l}.{ib}{ct}"] + 1)
                    if dst is y and ib == 0 and ct == 0:
                        dve.wait_ge(y_free, b + 1)
                    v.scalar_tensor_tensor(out=dst[:, ct, sl], in0=acc[:, ct, :], scalar=bias(ct),
                                           in1=base[:, ct, sl], op0=ALU.add, op1=ALU.add).then_inc(acc_read, 1)
                    if dst is not y and l == "L0":
                        wait_acc_read(dve, b, f"{l}.{ib}{ct}")
                        ins = v.bn_stats(gn_stats[:, ct, ib, :], dst[:, ct, sl])
                        if ib == NB - 1 and ct == CT - 1:
                            then(b, ins)

                row_max(0)
                for ti in range(NT):
                    if ti + 1 < NT:
                        row_max(ti + 1)
                    scale(ti)
                    if ti == 6:
                        residual(0, 0)
                residual(0, 1)
                residual(1, 0)
                residual(1, 1)

            def group_normed(b, l, dst):
                n = 1 if l == "L1" else 2
                r = norm_no[f"{l}.gn"]
                v.memset(idle_dve[:, r:r + 1], 0.0)
                v.bn_aggr(gn_mv[:, 0, :], gn_stats[:, 0, :, :].rearrange("p h s -> p (h s)"))
                then(b, v.bn_aggr(gn_mv[:, 1, :], gn_stats[:, 1, :, :].rearrange("p h s -> p (h s)")))
                mean, var = gn_mv[:, :, 0], gn_mv[:, :, 1]
                then(b, v.tensor_tensor(gn_sq[:, :], mean, mean, ALU.mult))
                v.tensor_copy(gn_in[:, :, 0], mean)
                v.tensor_tensor(gn_in[:, :, 1], gn_sq[:, :], var, ALU.add).then_inc(gn_in_ready, 1)
                wait_filled(dve, b, f"{l}.gn")
                v.tensor_copy(gn_out[:, :, :].rearrange("p c s -> p (c s)"),
                              slot(f"{l}.gn")[:, 0, 0:2 * CT]).then_inc(dve_read, 1)
                wait_read(dve, b, f"{l}.gn")
                gmean, gsq = gn_out[:, :, 0], gn_out[:, :, 1]
                then(b, v.tensor_tensor(gn_sq[:, :], gmean, gmean, ALU.mult))
                r = norm_no[f"{l}.gn"]
                v.scalar_tensor_tensor(out=var_eps[:, r, 0:CT], in0=gsq, scalar=EPS_GN, in1=gn_sq[:, :],
                                       op0=ALU.add, op1=ALU.subtract).then_inc(var_ready, 1)
                dve.wait_ge(rstd_ready, b * NORMS + r + 1)
                then(b, v.tensor_tensor(gn_sc[:, :], rstd[:, r, 0:CT], vecs[:, VECS.index(f"{l}_g"), :], ALU.mult))
                then(b, v.tensor_tensor(gn_msc[:, :], gmean, gn_sc[:, :], ALU.mult))
                v.tensor_tensor(gn_nb[:, :], vecs[:, VECS.index(f"{l}_b"), :], gn_msc[:, :],
                                ALU.subtract).then_inc(gn_coef_ready, 1)
                dve.wait_ge(gn_coef_ready, b * 2 + n)
                v.tensor_scalar(h[:, 0, :], x[:, 0, :], gn_sc[:, 0:1], gn_nb[:, 0:1], ALU.mult,
                                ALU.add).then_inc(h_dve, 1)
                for m in range(CT):
                    wait_filled(dve, b, f"{l}.k{m}")
                    v.tensor_scalar(k[:, m, :], flat(f"{l}.k{m}"), vec(f"{l}_bk", m), None,
                                    ALU.add).then_inc(dve_read, 1)
                wait_filled(dve, b, f"{l}.v0")
                v.tensor_copy(vt[:, 0:TPH, :].rearrange("p t c -> p (t c)"), flat(f"{l}.v0")).then_inc(dve_read, 1)
                full_attention(b, l, x, lambda ct: bvo[l][:, ct:ct + 1], dst)

            def layer_norm(b, name, src, dst, hf, signal):
                r = norm_no[name]
                tiles = range(hf * TPH, (hf + 1) * TPH)
                for i, ti in enumerate(tiles):
                    ins = v.bn_stats(ln_stats[:, r, i, :], src[:, ti, :])
                then(b, ins)
                v.memset(idle_dve[:, r:r + 1], 0.0)
                for i in range(TPH):
                    ins = v.bn_aggr(ln_mv[:, r, i, :], ln_stats[:, r, i, :])
                then(b, ins)
                v.tensor_scalar(var_eps[:, r, :], ln_mv[:, r, :, 1], EPS_LN, None, ALU.add).then_inc(var_ready, 1)
                dve.wait_ge(rstd_ready, b * NORMS + r + 1)
                for i, ti in enumerate(tiles):
                    ins = v.tensor_scalar(dst[:, ti, :], src[:, ti, :], ln_mv[:, r, i, 0:1],
                                          rstd[:, r, i:i + 1], ALU.subtract, ALU.mult)
                if signal:
                    ins.then_inc(ln_ready, 1)
                else:
                    then(b, ins)

            def causal_layer(b):
                for hf in range(NB):
                    wait_read(dve, b, f"L2.xt{hf}")
                    layer_norm(b, f"L2.ln1.{hf}", xs, an, hf, True)
                wait_filled(dve, b, "L2.k")
                v.tensor_copy(k[:, 0, :], flat("L2.k")).then_inc(dve_read, 1)
                wait_filled(dve, b, "L2.vt")
                v.tensor_copy(vT2[0:2 * DH, :], slot("L2.vt")[0:2 * DH, 0, :]).then_inc(dve_read, 1)
                wait_filled(dve, b, "L2.v")
                v.tensor_copy(v2[:, :, :].rearrange("p (f i) d -> p i f d", f=NB),
                              slot("L2.v")[:, 0, :].rearrange("p (i f d) -> p i f d", i=TPH, d=DH)[:, :, 0:NB, :]
                              ).then_inc(dve_read, 1)

                for e in schedule:
                    if e[0] == "max":
                        _, kk, ti, ch, lo, hi, pair = e
                        n = hi - lo
                        name = event_name(e)
                        i = ti % TPH
                        cols = max_cols[:, kk % 2, i, 2 * DH * pair:2 * DH * (pair + 1):DH]
                        part = part_max[:, i, :, 2 * pair:2 * pair + 2]
                        wait_filled(dve, b, name)
                        if hi == (ti + 1) * P:
                            d = slot(name)[:, :, n - P:n]
                            then(b, v.tensor_tensor(d, d, causal.unsqueeze(1).broadcast_to([P, 2, P]), ALU.add))
                        whole = ti < TPH
                        ins = v.tensor_reduce(cols if whole else part[:, ch, :], slot(name)[:, :, 0:n], AX_X,
                                              ALU.max, negate=True)
                        ins.then_inc(dve_read, 1)
                        if ch == 1:
                            wait_read(dve, b, name)
                            ins = v.tensor_tensor(cols, part[:, 0, :], part[:, 1, :], ALU.min)
                            if i == TPH - 1 and pair == 1:
                                ins.then_inc(max_ready, 1)
                    elif e[0] == "values":
                        _, kk, jt, step = e
                        hg, ib = blocks[kk]
                        if jt == TPH * (ib + 1) - 1:
                            dve.wait_ge(acc_filled, b * ACCS + acc_no[f"L2.{kk}"] + 1)
                            then(b, v.reciprocal(inv_den[:, :], acc[:, 1, :]))
                            v.tensor_tensor(heads_out[:, hg, ib * HALF:(ib + 1) * HALF], acc[:, 0, :],
                                            inv_den[:, :], ALU.mult).then_inc(acc_read, 1)

                def row(i):
                    return rows[:, i, :].unsqueeze(1).broadcast_to([P, TPH, C])

                def four(name):
                    return slot(name).rearrange("p b (s c) -> p (b s) c", c=C)

                for hf in (1, 0):
                    ts = slice(hf * TPH, (hf + 1) * TPH)
                    wait_filled(dve, b, f"L2.wo{hf}")
                    v.tensor_tensor(xs[:, ts, :], four(f"L2.wo{hf}"), xs[:, ts, :], ALU.add).then_inc(dve_read, 1)
                    wait_read(dve, b, f"L2.wo{hf}")
                    layer_norm(b, f"L2.ln2.{hf}", xs, xs, hf, False)
                    then(b, v.tensor_tensor(av[:, ts, :], xs[:, ts, :], row(0), ALU.mult))
                    then(b, v.tensor_tensor(av[:, ts, :], av[:, ts, :], row(1), ALU.add))
                    layer_norm(b, f"L2.f1.{hf}", av, an, hf, True)
                for hf in (1, 0):
                    ts = slice(hf * TPH, (hf + 1) * TPH)
                    wait_filled(dve, b, f"L2.w1_{hf}")
                    v.tensor_tensor(an[:, ts, :], four(f"L2.w1_{hf}"), row(2), ALU.add).then_inc(dve_read, 1)
                    wait_read(dve, b, f"L2.w1_{hf}")
                    layer_norm(b, f"L2.f2.{hf}", an, an, hf, True)
                for hf in (1, 0):
                    wait_read(dve, b, f"L2.w2_{hf}")
                    for c in range(CT):
                        ins = v.bn_stats(gn_stats[:, c, hf, :], x[:, c, hf * HALF:(hf + 1) * HALF])
                then(b, ins)

            with dve.Fori(0, B) as b:
                steps[0] = 0
                wait_filled(dve, b, "L0.k")
                v.tensor_scalar(k[:, 0, :], flat("L0.k"), bqk0[:, 1:2], None, ALU.add).then_inc(dve_read, 1)
                wait_filled(dve, b, "L0.v0")
                v.tensor_copy(vt[:, 0:TPH, :].rearrange("p t c -> p (t c)"), flat("L0.v0")).then_inc(dve_read, 1)
                full_attention(b, "L0", xin, lambda ct: bv0[:, ct:ct + 1], x)
                group_normed(b, "L1", x)
                causal_layer(b)
                group_normed(b, "L3", y)
            assert steps[0] == DVE_STEPS, steps[0]


def kernel(**inputs):
    import numpy as _np
    import concourse.bacc as _bacc
    from concourse import mybir as _mybir
    from concourse.bass_utils import run_bass_kernel_spmd as _run

    i = {n: _np.asarray(a) for n, a in inputs.items()}
    cols = [i["L0_conv_bv"]] + [i[f"L1_conv_{n}"] for n in ("gn_scale", "gn_bias", "bq", "bk", "bv", "bo")]
    cols += [i[f"L2_conv_{n}"] for n in ("ln1_g", "ln1_b", "ff_ln1_g", "ff_ln1_b", "ff_ln2_g", "ff_ln2_b", "ff_b2")]
    cols += [i[f"L3_conv_{n}"] for n in ("norm_g", "norm_b", "bq", "bk", "bv", "bo")]
    group = C // 32
    channel = _np.arange(P)
    consts = _np.stack([
        _np.eye(P, dtype=_np.float32),
        (channel[:, None] // group == channel[None, :] // group).astype(_np.float32) / _np.float32(group),
        _np.where(channel[None, :] > channel[:, None], _np.float32(-3e38), _np.float32(0)),
    ])
    arrays = {
        "x": i["x"],
        "L0_WqT": i["L0_conv_Wq"].T, "L0_WkT": i["L0_conv_Wk"].T, "L0_WvT": i["L0_conv_Wv"].T,
        "L0_bq": i["L0_conv_bq"].reshape(DH, 1), "L0_bk": i["L0_conv_bk"].reshape(DH, 1),
        "gamma": i["L0_conv_gamma"],
        "vecs": _np.stack(cols).reshape(len(VECS), CT, P).transpose(2, 0, 1),
        "rows": _np.stack([i["L2_conv_ln2_g"], i["L2_conv_ln2_b"], i["L2_conv_ff_b1"]]),
        "consts": consts.transpose(1, 0, 2),
        "L2_wq": i["L2_conv_wq"], "L2_wkv": i["L2_conv_wkv"], "L2_wo": i["L2_conv_wo"],
        "L2_w1": i["L2_conv_ff_w1"], "L2_w2": i["L2_conv_ff_w2"],
    }
    for l in ("L1", "L3"):
        arrays[f"{l}_wqT"] = i[f"{l}_conv_wq"].T
        arrays[f"{l}_wkT"] = i[f"{l}_conv_wk"].T
        arrays[f"{l}_wv"] = i[f"{l}_conv_wv"]
        arrays[f"{l}_woT"] = i[f"{l}_conv_wo"].T
    arrays = {f"{n}_dram": _np.ascontiguousarray(a) for n, a in arrays.items()}
    nc = _bacc.Bacc("TRN2", target_bir_lowering=False, num_devices=1)
    tensors = {n[:-5]: nc.dram_tensor(n, a.shape, _mybir.dt.from_np(a.dtype), kind="ExternalInput").ap()
               for n, a in arrays.items()}
    tensors["out"] = nc.dram_tensor("out_dram", (B, C, 32, 32), _mybir.dt.float32, kind="ExternalOutput").ap()
    build(nc, tensors)
    r = _run(nc, [arrays], core_ids=[0])
    return r.results[0]["out_dram"]
```

```python
from contextlib import ExitStack

import concourse.bass as bass
from concourse import mybir

F32 = mybir.dt.float32
F32R = mybir.dt.float32r
ALU = mybir.AluOpType
ACT = mybir.ActivationFunctionType
AX_X = mybir.AxisListType.X

P = 128
B, C, N = 4, 256, 1024
CT = C // P
NT = N // P
HALF = 512
NB = N // HALF
TPH = HALF // P
HEADS, DH = 8, 32
HG = 2
EPS_GN, EPS_LN = 1e-6, 1e-5
SLOTS = 3

VECS = ["L0_bv", "L1_g", "L1_b", "L1_bq", "L1_bk", "L1_bv", "L1_bo", "L2_ln1_g", "L2_ln1_b",
        "L2_f1_g", "L2_f1_b", "L2_f2_g", "L2_f2_b", "L2_b2", "L3_g", "L3_b", "L3_bq", "L3_bk",
        "L3_bv", "L3_bo"]
ROWS = ["ln2_g", "ln2_b", "ff_b1"]

START = 1

DVE_STEPS = 108


def causal_blocks():
    return [(0, 0), (0, 1), (1, 1), (1, 0)]


def causal_schedule():
    blocks = causal_blocks()

    def max_events(k):
        hg, ib = blocks[k]
        out = []
        for t in range(TPH * ib, TPH * (ib + 1)):
            end = (t + 1) * P
            for ch, (lo, hi) in enumerate([(0, end)] if end <= HALF else [(0, HALF), (HALF, end)]):
                out.append([("max", k, t, ch, lo, hi, pair) for pair in range(2)])
        return out

    events = [e for two in max_events(0) for e in two] + [("shift", 0)]
    pending = None
    step = 0
    for k, (hg, ib) in enumerate(blocks):
        ahead = max_events(k + 1) if k + 1 < len(blocks) else []
        tiles = TPH * (ib + 1)
        done = 0
        for jt in range(tiles):
            events += [("exp", k, jt, pair, step) for pair in range(2)]
            if pending:
                events.append(pending)
            pending = ("values", k, jt, step)
            step += 1
            upto = len(ahead) * (jt + 1) // tiles
            events += [e for two in ahead[done:upto] for e in two]
            done = upto
        if ahead:
            events.append(("shift", k + 1))
    return events + [pending]


def attention_units(layer):
    out = [(f"{layer}.s0", "act"), (f"{layer}.s1", "act")]
    for t in range(NT):
        out.append((f"{layer}.t{t}", "dve"))
        if t + 2 < NT:
            out.append((f"{layer}.s{t + 2}", "act"))
    return out


def event_name(e):
    return "L2." + ".".join(map(str, e[:3] if e[0] == "values" else e[:4] + e[-1:]))


def ring_units():
    units = [("L0.q", "dve"), ("L0.k", "dve"), ("L0.v0", "dve"), ("L0.v1", "dve")]
    units += attention_units("L0")
    for layer in ("L1", "L3"):
        if layer == "L3":
            units += [("L2.xt0", "act"), ("L2.xt1", "act"), ("L2.xn0", "dve"), ("L2.xn1", "dve"),
                      ("L2.q0", "dve"), ("L2.kv", "dve"), ("L2.q1", "dve"), ("L2.v", "dve")]
            for e in causal_schedule():
                if e[0] != "values":
                    units.append((event_name(e), "dve" if e[0] == "max" else "act"))
            units += [("L2.wo1", "dve"), ("L2.wo0", "dve"), ("L2.ta1", "dve"), ("L2.w1_1", "dve"),
                      ("L2.ta0", "dve"), ("L2.w1_0", "dve"), ("L2.tg1", "act"), ("L2.w2_1", "act"),
                      ("L2.tg0", "act"), ("L2.w2_0", "act")]
        units += [(f"{layer}.gn", "dve")]
        units += [(f"{layer}.{u}", "dve") for u in ("q0", "k0", "q1", "k1", "v0", "v1")]
        units += attention_units(layer)
    return units


def split_units(units):
    whole = ("gn", "L2.v", "wo", "w1", "max")
    return [n for n, eng in units if eng == "dve" and not any(
        n.endswith(w) or f".{w}" in n for w in whole)]


def accumulator_uses():
    full = [(ib, ct) for ib in range(NB) for ct in range(CT)]
    return ([(f"L0.{ib}{ct}", (ct,)) for ib, ct in full] + [(f"L1.{ib}{ct}", (ct,)) for ib, ct in full]
            + [(f"L2.{k}", (0, 1)) for k in range(len(causal_blocks()))]
            + [(f"L3.{ib}{ct}", (ct,)) for ib, ct in full])


def build(nc, t):
    units = ring_units()
    number = {name: u for u, (name, _) in enumerate(units)}
    reader = dict(units)
    U = len(units)
    rank, total = {}, {"act": 0, "dve": 0}
    for name, eng in units:
        total[eng] += 1
        rank[name] = total[eng]
    halves = split_units(units)
    half_no = {name: i for i, name in enumerate(halves)}
    SPLITS = len(halves)
    acc_uses = accumulator_uses()
    acc_no = {name: i for i, (name, _) in enumerate(acc_uses)}
    ACCS = len(acc_uses)
    schedule = causal_schedule()
    blocks = causal_blocks()
    norms = ["L1.gn", "L2.ln1.0", "L2.ln1.1", "L2.ln2.1", "L2.f1.1", "L2.ln2.0", "L2.f1.0",
             "L2.f2.1", "L2.f2.0", "L3.gn"]
    norm_no = {name: i for i, name in enumerate(norms)}
    NORMS = len(norms)
    diagonal = [e for e in schedule if e[0] == "exp" and e[2] >= TPH * blocks[e[1]][1]]
    DIAG = len(diagonal)
    last_max = {e[1]: e for e in schedule if e[0] == "max"}
    first_max = {hg: next(e for e in schedule if e[0] == "max" and blocks[e[1]][0] == hg) for hg in range(HG)}
    diag_no = {event_name(e): i for i, e in enumerate(diagonal)}

    with ExitStack() as ctx:
        def sem(name):
            return ctx.enter_context(nc.semaphore(name))

        top = [(nc.sbuf_base + 31) // 32 * 32]

        def region(kib):
            at = top[0]
            top[0] += kib * 1024
            return at

        def place(name, shape, at, dtype=F32):
            size = 4
            for d in shape[1:]:
                size *= d
            return nc.alloc_sbuf_tensor_at(name, shape, dtype, offset=at), at + size

        def shared(name, shape, at, dtype=F32):
            return place(name, shape, at, dtype)[0]

        def sb(name, shape, dtype=F32):
            tensor, end = place(name, shape, top[0], dtype)
            top[0] = (end + 31) // 32 * 32
            return tensor

        def pair(name, shape, at=None):
            size = 4
            for d in shape[1:]:
                size *= d
            if at is None:
                return sb(f"{name}_hi", shape, F32R), sb(f"{name}_lo", shape, F32R)
            return shared(f"{name}_hi", shape, at, F32R), shared(f"{name}_lo", shape, at + size, F32R)

        KIB = 1024
        r_xin, r_x, r_q, r_k, r_v = region(8), region(8), region(16), region(16), region(16)
        r_p, r_t, r_s = region(8), region(64), region(8)
        xin = shared("xin", [P, CT, N], r_xin)
        x = shared("x", [P, CT, N], r_x)
        h = pair("h", [P, CT, N], r_t)
        q, k = pair("q", [P, CT, N], r_q), pair("k", [P, CT, N], r_k)
        qs0 = shared("qs0", [P, N], r_q, F32R)
        ks0 = shared("ks0", [P, N], r_k, F32R)
        vt = pair("vt", [P, NT, C], r_v)
        probs = shared("probs", [P, 2, N], r_p)
        probsT = pair("probsT", [P, NB, NT, HALF], r_t)
        h_full = shared("h_full", [P, CT, N], r_p)
        y = shared("y", [P, CT, N], r_k + 8 * KIB)
        q2 = pair("q2", [P, HG, N], r_q)
        ks = shared("ks", [P, N], r_k, F32R)
        max_rows = shared("max_rows", [P, 2, HALF], r_k + 4 * KIB, F32R)
        max_cols = shared("max_cols", [P, 2, TPH, P], r_k + 8 * KIB)
        inv_den = shared("inv_den", [P, HALF], r_k + 12 * KIB)
        vT2 = shared("vT2", [P, N // 2], r_k + 14 * KIB)
        heads_out = pair("heads_out", [P, HG, N], r_v)
        cprobs = shared("cprobs", [P, 4, 4, HALF], r_t)
        qs = shared("qs", [P, HEADS, N], r_t + 32 * KIB, F32R)
        an = shared("an", [P, NT, C], r_p)
        xs = shared("xs", [P, NT, C], r_s)
        gelu = x
        act2 = pair("act2", [P, CT, N], r_q)

        raw_at = [r_t]

        def raw(name, shape):
            tensor, raw_at[0] = place(name, shape, raw_at[0])
            return tensor

        raw_qk0 = raw("raw_qk0", [P, 2, CT, 4, DH])
        raw_v0 = raw("raw_v0", [P, CT, C])
        raws = {}
        for l in ("L1", "L3"):
            for w in ("wqT", "wkT", "wv", "woT"):
                raws[l, w] = raw(f"raw_{l}_{w}", [P, CT, C])
        raw_q2, raw_kv2 = raw("raw_q2", [P, CT, C]), raw("raw_kv2", [P, CT, 4, DH])
        raw_o2, raw_w1, raw_w2 = raw("raw_o2", [P, HG, C]), raw("raw_w1", [P, CT, C]), raw("raw_w2", [P, CT, C])
        f1b_wide = raw("f1b_wide", [P, CT, P])

        wqk0, wv0 = pair("wqk0", [P, 2, CT, P]), pair("wv0", [P, CT, C])
        wq, wk, wvo, bqs, bvo = {}, {}, {}, {}, {}
        for l in ("L1", "L3"):
            wq[l], wk[l] = pair(f"{l}_wq", [P, CT, C]), pair(f"{l}_wk", [P, CT, C])
            wvo[l] = pair(f"{l}_wvo", [P, CT, C])
            bqs[l] = sb(f"{l}_bqs", [P, CT])
            bvo[l] = sb(f"{l}_bvo", [P, CT])
        wq2, wkv2 = pair("wq2", [P, CT, C]), pair("wkv2", [P, CT, P])
        wo2, ffw1, ffw2 = pair("wo2", [P, HG, C]), pair("ffw1", [P, CT, C]), pair("ffw2", [P, CT, C])
        bq2, bkv2 = sb("bq2", [P, HG]), sb("bkv2", [P, 1])
        bqk0 = sb("bqk0", [P, 2])
        gamma = sb("gamma", [P, 1])
        vecs = sb("vecs", [P, len(VECS), CT])
        rows = sb("rows", [P, len(ROWS), C])
        consts = sb("consts", [P, 3, P])
        ones = sb("ones", [P, DH])
        half_neg = sb("half_neg", [P, 4])
        ident, group_mean, causal = consts[:, 0, :], consts[:, 1, :], consts[:, 2, :]

        v2 = sb("v2", [P, NT, DH])
        neg_max, row_sum, row_inv = sb("neg_max", [P, NT]), sb("row_sum", [P, NT]), sb("row_inv", [P, NT])
        gn_stats = sb("gn_stats", [P, CT, NB, 6])
        gn_mv, gn_in, gn_out = sb("gn_mv", [P, CT, 2]), sb("gn_in", [P, CT, 2]), sb("gn_out", [P, CT, 2])
        gn_sq, gn_sc, gn_msc, gn_nb = (sb(f"gn_{s}", [P, CT]) for s in ("sq", "sc", "msc", "nb"))
        var_eps, rstd = sb("var_eps", [P, NORMS, 4]), sb("rstd", [P, NORMS, 4])
        ln_stats, ln_mv = sb("ln_stats", [P, NORMS, TPH, 6]), sb("ln_mv", [P, NORMS, TPH, 2])
        part_max = sb("part_max", [P, TPH, 2, 4])
        cmax = sb("cmax", [P, 2, TPH, 4])
        cmax_hi = sb("cmax_hi", [P, 2, TPH, 4], F32R)
        idle_act = sb("idle_act", [P, 1])
        idle_pool, idle_dve = sb("idle_pool", [P, DIAG + 1]), sb("idle_dve", [P, NORMS])
        assert top[0] <= nc.sbuf_usable_end, (top[0], nc.sbuf_usable_end)

        def causal_probs(step, two, n):
            return cprobs[:, step % 4, 2 * two:2 * two + 2, 0:n]

        ring = ctx.enter_context(nc.psum_tensor("ring", [P, SLOTS, 2, HALF], F32))
        acc = ctx.enter_context(nc.psum_tensor("acc", [P, 2, HALF], F32))

        weights_in = sem("weights_in")
        x_in = sem("x_in")
        y_out = sem("y_out")
        stack_in = [sem(f"stack_in{g}") for g in range(HG)]
        shift_in = sem("shift_in")
        y_free = sem("y_free")
        ring_filled = sem("ring_filled")
        hi_ready = sem("hi_ready")
        act_read = sem("act_read")
        dve_read = sem("dve_read")
        acc_filled = sem("acc_filled")
        acc_read = sem("acc_read")
        row_max_ready = sem("row_max_ready")
        probs_scaled = sem("probs_scaled")
        gn_in_ready = sem("gn_in_ready")
        gn_coef_ready = sem("gn_coef_ready")
        h_hi, h_lo = sem("h_hi"), sem("h_lo")
        gelu_ready = sem("gelu_ready")
        act2_ready = sem("act2_ready")
        out_ready = sem("out_ready")
        var_ready = sem("var_ready")
        rstd_ready = sem("rstd_ready")
        ln_ready = sem("ln_ready")
        max_ready = sem("max_ready")
        one_rows = sem("one_rows")
        diag_masked = sem("diag_masked")
        dve_step = sem("dve_step")
        prep_mm, prep_hi, prep_step = sem("prep_mm"), sem("prep_hi"), sem("prep_step")
        prep_done, setup = sem("prep_done"), sem("setup")

        unit_slot = {name: number[name] % SLOTS for name in number}
        LAYER3 = {"L0": 0, "L1": 1, "L3": 2}

        def slot(name):
            return ring[:, unit_slot[name], :, :]

        def flat(name):
            return slot(name).rearrange("p b n -> p (b n)")

        def wait_read(eng, b, name):
            e = reader[name]
            eng.wait_ge(act_read if e == "act" else dve_read, b * total[e] + START + rank[name])

        def wait_filled(eng, b, name):
            eng.wait_ge(ring_filled, b * U + (number[name] + 1))

        def wait_hi(eng, b, name):
            eng.wait_ge(hi_ready, b * SPLITS + (half_no[name] + 1))

        def wait_acc_read(eng, b, name):
            eng.wait_ge(acc_read, b * ACCS + START + (acc_no[name] + 1))

        def vec(name, ct):
            return vecs[:, VECS.index(name), ct:ct + 1]

        LOADS = [
            (vecs[:, :, :], t["vecs"]),
            (consts[:, :, :], t["consts"]),
            (gamma[:, :], t["gamma"].partition_broadcast(P)),
            (raw_v0[:, :, :], t["L0_WvT"].rearrange("(c p) o -> p c o", p=P)),
        ]
        for g in range(4):
            for i, w in enumerate(("L0_WqT", "L0_WkT")):
                LOADS.append((raw_qk0[:, i, :, g, :], t[w].rearrange("(c p) m -> p c m", p=P)))
                LOADS.append((bqk0[DH * g:DH * (g + 1), i:i + 1], t[("L0_bq", "L0_bk")[i]]))
            col = DH if g == 3 else 0
            LOADS.append((raw_kv2[:, :, g, :], t["L2_wkv"][:, col:col + DH].rearrange("(c p) o -> p c o", p=P)))
        for l in ("L1", "L3"):
            for w in ("wqT", "wkT", "wv", "woT"):
                LOADS.append((raws[l, w][:, :, :], t[f"{l}_{w}"].rearrange("(c p) o -> p c o", p=P)))
        for dst, w in ((raw_q2, "wq"), (raw_o2, "wo"), (raw_w1, "w1"), (raw_w2, "w2")):
            LOADS.append((dst[:, :, :], t[f"L2_{w}"].rearrange("(c p) o -> p c o", p=P)))
        for i in range(len(ROWS)):
            LOADS.append((rows[:, i, :], t["rows"][i, :].partition_broadcast(P)))
        ALL_LOADED = 16 * len(LOADS)

        SPLIT = [(raw_qk0[:, i, c, :, :].rearrange("p g d -> p (g d)"), wqk0, (i, c), None, 1.0)
                 for i in range(2) for c in range(CT)]
        for c in range(CT):
            SPLIT += [(raw_v0[:, c, :], wv0, (c,), gamma[:, 0:1], 1.0),
                      (raw_q2[:, c, :], wq2, (c,), vec("L2_ln1_g", c), DH ** -0.5),
                      (raw_kv2[:, c, :, :].rearrange("p g d -> p (g d)"), wkv2, (c,), vec("L2_ln1_g", c), 1.0),
                      (raw_o2[:, c, :], wo2, (c,), None, 1.0),
                      (raw_w1[:, c, :], ffw1, (c,), vec("L2_f1_g", c), 1.0),
                      (raw_w2[:, c, :], ffw2, (c,), None, 1.0)]
            for l in ("L1", "L3"):
                SPLIT += [(raws[l, "wqT"][:, c, :], wq[l], (c,), None, C ** -0.5),
                          (raws[l, "wkT"][:, c, :], wk[l], (c,), None, 1.0)]

        def part(two, which, idx):
            ap = two[which]
            return ap[:, idx[0], idx[1], :] if len(idx) == 2 else ap[:, idx[0], :]

        block = ctx.enter_context(nc.Block())

        @block.sync
        def _(sp):
            x_dram = t["x"].rearrange("b (c p) h w -> b p c (h w)", p=P)
            y_dram = t["out"].rearrange("b (c p) h w -> b p c (h w)", p=P)
            sp.dma_start(xin[:, :, :], x_dram[0]).then_inc(x_in, 16)
            for dst, src in LOADS:
                sp.dma_start(dst, src).then_inc(weights_in, 16)
            sp.sem_inc(y_free, 1)

            def moves(b):
                for hg in range(HG):
                    wait_read(sp, b, f"L2.q{hg}")
                    for a in range(4):
                        for g, src in enumerate((q2[0], q2[0], q2[1])):
                            sp.dma_start(qs[DH * g:DH * (g + 1), 4 * hg + a, :].bitcast(F32),
                                         src[DH * a:DH * (a + 1), hg, :].bitcast(F32)).then_inc(stack_in[hg], 16)
                for kk, (hg, ib) in enumerate(blocks):
                    wait_read(sp, b, event_name(("shift", kk)))
                    for a in range(4):
                        sp.dma_start(qs[3 * DH:3 * DH + 2, 4 * hg + a, ib * HALF:(ib + 1) * HALF].bitcast(F32),
                                     max_rows[DH * a:DH * a + 2, kk % 2, :].bitcast(F32)).then_inc(shift_in, 16)
                for ib in range(NB):
                    wait_acc_read(sp, b, f"L3.{ib}{CT - 1}")
                    sl = slice(ib * HALF, (ib + 1) * HALF)
                    sp.dma_start(y_dram[b][:, :, sl], y[:, :, sl]).then_inc(y_out, 16)
                sp.wait_ge(y_out, b * (16 * NB) + 16 * NB)
                sp.sem_inc(y_free, 1)

            with sp.Fori(0, B - 1) as b:
                wait_acc_read(sp, b, f"L0.{NB - 1}{CT - 1}")
                sp.dma_start(xin[:, :, :], x_dram[b + 1]).then_inc(x_in, 16)
                moves(b)
            moves(B - 1)

        @block.gpsimd
        def _(pool):
            pool.memset(ones[:, :], 1.0).then_inc(setup, 1)
            pool.memset(half_neg[:, :], -0.5).then_inc(setup, 1)
            pool.wait_ge(setup, 2)

            def root(b, name):
                n = norm_no[name]
                w = CT if name.endswith("gn") else TPH
                pool.wait_ge(var_ready, b * NORMS + (n + 1))
                pool.tensor_tensor(rstd[:, n, 0:w], var_eps[:, n, 0:w], half_neg[:, 0:w],
                                   ALU.pow).then_inc(rstd_ready, 1)

            with pool.Fori(0, B) as b:
                for name in norms[:3]:
                    root(b, name)
                for i, e in enumerate(diagonal):
                    _, kk, jt, two, step = e
                    wait_read(pool, b, event_name(e))
                    d = causal_probs(step, two, P)
                    if i:
                        pool.tensor_tensor(idle_pool[:, i:i + 1], half_neg[:, 0:1], half_neg[:, 0:1], ALU.mult)
                    else:
                        pool.tensor_tensor(idle_pool[:, DIAG:DIAG + 1], half_neg[:, 0:1], half_neg[:, 0:1], ALU.mult)
                    pool.affine_select(out=d, in_=d, pattern=[[0, 2], [1, P]], compare_op=ALU.is_ge,
                                       fill=0.0, base=0, channel_multiplier=-1).then_inc(diag_masked, 1)
                for name in norms[3:]:
                    root(b, name)

        @block.tensor
        def _(pe):
            mm = nc.tensor.matmul
            PASSES = ((0, 0), (0, 1), (1, 0))

            def open_unit(b, name):
                u = number[name]
                if u >= SLOTS:
                    wait_read(pe, b, units[u - SLOTS][0])
                else:
                    pe.wait_ge(act_read, b * total["act"] + START)
                    pe.wait_ge(dve_read, b * total["dve"] + START)
                return slot(name)

            def open_acc(b, name):
                i = acc_no[name]
                before = [j for j in range(i) if set(acc_uses[j][1]) & set(acc_uses[i][1])]
                pe.wait_ge(acc_read, b * ACCS + START + (before[-1] + 1 if before else 0))

            def product(out, terms, first=True, last=True):
                every = [(w[i], m[j]) for w, m in terms for i, j in PASSES]
                for n, (w, m) in enumerate(every):
                    ins = mm(out, w, m, start=first and n == 0, stop=last and n == len(every) - 1)
                return ins

            pe.wait_ge(weights_in, ALL_LOADED)
            for l, out in (("L1", acc), ("L3", ring[:, 0, :, :])):
                for ci in range(CT):
                    for m in range(CT):
                        mm(out[:, ci, 0:C], raws[l, "wv"][:, m, ci * P:(ci + 1) * P], raws[l, "woT"][:, m, :],
                           start=m == 0, stop=m == CT - 1)
                for co in range(CT):
                    for m in range(CT):
                        last = mm(out[:, co, C:C + 1], raws[l, "woT"][:, m, co * P:(co + 1) * P],
                                  vec(f"{l}_bv", m), start=m == 0, stop=m == CT - 1)
                last.then_inc(prep_mm, 1)
            out = ring[:, 1, 0, :]
            for hg in range(HG):
                for c in range(CT):
                    mm(out[:, hg:hg + 1], raw_q2[:, c, hg * P:(hg + 1) * P], vec("L2_ln1_b", c),
                       start=c == 0, stop=c == CT - 1)
            for c in range(CT):
                mm(out[:, 2:3], raw_kv2[:, c, :, :].rearrange("p g d -> p (g d)"), vec("L2_ln1_b", c),
                   start=c == 0, stop=c == CT - 1)
            pe.wait_ge(prep_step, 1)
            for c in range(CT):
                last = mm(out[:, C:2 * C], f1b_wide[:, c, :], raw_w1[:, c, :], start=c == 0, stop=c == CT - 1)
            last.then_inc(prep_mm, 1)
            pe.wait_ge(prep_done, 1)
            pe.wait_ge(setup, 2)

            def project(b, name, w, src):
                o = open_unit(b, name)
                for hf in range(NB):
                    sl = slice(hf * HALF, (hf + 1) * HALF)
                    last = product(o[:, hf, :], [([w(i, c) for i in (0, 1)], [s[:, c, sl] for s in src])
                                                 for c in range(CT)])
                last.then_inc(ring_filled, 1)

            def token_project(b, name, src, w, t0):
                o = open_unit(b, name).rearrange("p b (s c) -> p (b s) c", c=C)
                for i in range(TPH):
                    sl = slice((t0 + i) * P, (t0 + i + 1) * P)
                    last = product(o[:, i, :], [([s[:, c, sl] for s in src], [u[:, c, :] for u in w])
                                                for c in range(CT)])
                last.then_inc(ring_filled, 1)

            def full_attention(b, l):
                def scores(ti):
                    o = open_unit(b, f"{l}.s{ti}")
                    ts = slice(ti * P, (ti + 1) * P)
                    for hf in range(NB):
                        keys = slice(hf * HALF, (hf + 1) * HALF)
                        if l == "L0":
                            last = mm(o[:, hf, :], qs0[:, ts], ks0[:, keys], start=True, stop=True)
                        else:
                            last = product(o[:, hf, :], [([s[:, c, ts] for s in q], [s[:, c, keys] for s in k])
                                                         for c in range(CT)])
                    last.then_inc(ring_filled, 1)

                def turn(ti):
                    o = open_unit(b, f"{l}.t{ti}").rearrange("p b (s n) -> p (b s) n", n=P)
                    pe.wait_ge(probs_scaled, b * (3 * NT) + LAYER3[l] * NT + ti + 1)
                    for j in range(NT):
                        last = nc.tensor.transpose(o[:, j, :], probs[:, ti % 2, j * P:(j + 1) * P], ident)
                    last.then_inc(ring_filled, 1)

                def values(ib, quarter):
                    ct, j0 = divmod(quarter * TPH, NT)
                    if j0 == 0:
                        open_acc(b, f"{l}.{ib}{ct}")
                    last = product(acc[:, ct, :], [([s[:, j, ct * P:(ct + 1) * P] for s in vt],
                                                    [s[:, ib, j, :] for s in probsT])
                                                   for j in range(j0, j0 + TPH)],
                                   first=j0 == 0, last=j0 + TPH == NT)
                    if j0 + TPH == NT:
                        last.then_inc(acc_filled, 1)

                scores(0)
                scores(1)
                for ti in range(NT):
                    turn(ti)
                    if ti + 2 < NT:
                        scores(ti + 2)
                    if ti == TPH:
                        wait_read(pe, b, f"{l}.v1")
                        wait_read(pe, b, f"{l}.t{TPH - 1}")
                    if ti >= TPH:
                        values(0, ti - TPH)
                wait_read(pe, b, f"{l}.t{NT - 1}")
                for quarter in range(TPH):
                    values(1, quarter)

            def group_normed(b, l):
                n = 1 if l == "L1" else 2
                pe.wait_ge(gn_in_ready, b * 2 + n)
                o = open_unit(b, f"{l}.gn")
                mm(o[:, 0, 0:2 * CT], group_mean, gn_in[:, :, :].rearrange("p c s -> p (c s)"),
                   start=True, stop=True).then_inc(ring_filled, 1)
                pe.wait_ge(h_lo, b * 3 + n + 1)
                for m in range(CT):
                    ms = slice(m * P, (m + 1) * P)
                    project(b, f"{l}.q{m}", lambda i, c: wq[l][i][:, c, ms], h)
                    project(b, f"{l}.k{m}", lambda i, c: wk[l][i][:, c, ms], h)
                for i in range(2):
                    token_project(b, f"{l}.v{i}", h, wvo[l], i * TPH)
                wait_read(pe, b, f"{l}.k1")
                full_attention(b, l)

            def causal_layer(b):
                for hf in range(NB):
                    wait_acc_read(pe, b, f"L1.{hf}{CT - 1}")
                    o = open_unit(b, f"L2.xt{hf}").rearrange("p b (s c n) -> p (b s) c n", c=CT, n=P)
                    for i in range(TPH):
                        ti = hf * TPH + i
                        for c in range(CT):
                            last = nc.tensor.transpose(o[:, i, c, :], x[:, c, ti * P:(ti + 1) * P], ident)
                    last.then_inc(ring_filled, 1)

                def turn_normed(name, hf, nth):
                    pe.wait_ge(ln_ready, b * 6 + nth)
                    o = open_unit(b, name)
                    for i in range(TPH):
                        for c in range(CT):
                            last = nc.tensor.transpose(o[:, c, i * P:(i + 1) * P],
                                                       an[:, hf * TPH + i, c * P:(c + 1) * P], ident)
                    last.then_inc(ring_filled, 1)

                turn_normed("L2.xn0", 0, 1)
                turn_normed("L2.xn1", 1, 2)
                wait_read(pe, b, "L2.xn1")
                project(b, "L2.q0", lambda i, c: wq2[i][:, c, 0:P], h)
                project(b, "L2.kv", lambda i, c: wkv2[i][:, c, :], h)
                project(b, "L2.q1", lambda i, c: wq2[i][:, c, P:2 * P], h)
                wait_read(pe, b, "L2.kv")
                o = open_unit(b, "L2.v").rearrange("p b (s n) -> p (b s) n", n=P)
                for i in range(NT):
                    last = nc.tensor.transpose(o[:, i, :], an[:, i // 2, (i % 2) * P:(i % 2 + 1) * P], ident)
                last.then_inc(ring_filled, 1)
                pe.wait_ge(one_rows, b + 1)

                for e in schedule:
                    kk = e[1]
                    hg, ib = blocks[kk]
                    if e[0] == "max":
                        _, _, ti, _, lo, hi, two = e
                        if e == first_max[hg]:
                            pe.wait_ge(stack_in[hg], b * (16 * 12) + 16 * 12)
                        o = open_unit(b, event_name(e))
                        for i in range(2):
                            last = mm(o[:, i, 0:hi - lo], qs[0:3 * DH, 4 * hg + 2 * two + i, ti * P:(ti + 1) * P],
                                      ks[0:3 * DH, lo:hi], start=True, stop=True)
                        last.then_inc(ring_filled, 1)
                    elif e[0] == "shift":
                        pe.wait_ge(max_ready, b * len(blocks) + kk + 1)
                        o = open_unit(b, event_name(e))
                        for i in range(TPH):
                            last = nc.tensor.transpose(o[:, 0, i * P:(i + 1) * P], max_cols[:, kk % 2, i, :], ident)
                        last.then_inc(ring_filled, 1)
                    elif e[0] == "exp":
                        _, _, jt, two, step = e
                        i0 = max(jt * P, ib * HALF)
                        n = (ib + 1) * HALF - i0
                        if jt == 0 and two == 0:
                            pe.wait_ge(shift_in, b * (64 * len(blocks)) + 64 * (kk + 1))
                        o = open_unit(b, event_name(e))
                        for i in range(2):
                            last = mm(o[:, i, 0:n], ks[0:3 * DH + 2, jt * P:(jt + 1) * P],
                                      qs[0:3 * DH + 2, 4 * hg + 2 * two + i, i0:i0 + n], start=True, stop=True)
                        last.then_inc(ring_filled, 1)
                    else:
                        _, _, jt, step = e
                        i0 = max(jt * P, ib * HALF)
                        n = (ib + 1) * HALF - i0
                        last_jt = TPH * (ib + 1) - 1
                        if jt == 0:
                            open_acc(b, f"L2.{kk}")
                            if kk == 0:
                                wait_read(pe, b, "L2.v")
                        name = event_name(("exp", kk, jt, 1, step))
                        if name in diag_no:
                            pe.wait_ge(diag_masked, b * DIAG + diag_no[name] + 1)
                        else:
                            wait_read(pe, b, name)
                        for bank, w in ((0, v2[:, jt, :]), (1, ones[:, 0:DH])):
                            for a in range(4):
                                last = mm(acc[DH * a:DH * (a + 1), bank, HALF - n:HALF], w,
                                          causal_probs(step, a // 2, n)[:, a % 2, :],
                                          start=jt == 0, stop=jt == last_jt)
                        if jt == last_jt:
                            last.then_inc(acc_filled, 1)

                for hf in (1, 0):
                    pe.wait_ge(out_ready, b * len(blocks) + (3 if hf else 4))
                    token_project(b, f"L2.wo{hf}", heads_out, wo2, hf * TPH)
                for n, hf in enumerate((1, 0)):
                    turn_normed(f"L2.ta{hf}", hf, 3 + n)
                    wait_read(pe, b, f"L2.ta{hf}")
                    token_project(b, f"L2.w1_{hf}", h, ffw1, hf * TPH)
                for n, hf in enumerate((1, 0)):
                    turn_normed(f"L2.tg{hf}", hf, 5 + n)
                    pe.wait_ge(act2_ready, b * 2 + n + 1)
                    o = open_unit(b, f"L2.w2_{hf}")
                    sl = slice(hf * HALF, (hf + 1) * HALF)
                    for co in range(CT):
                        cs = slice(co * P, (co + 1) * P)
                        product(o[:, co, :], [([w[:, c, cs] for w in ffw2], [a[:, c, sl] for a in act2])
                                              for c in range(CT)], last=False)
                        for i in range(TPH):
                            last = mm(o[:, co, i * P:(i + 1) * P], xs[:, hf * TPH + i, cs], ident,
                                      start=False, stop=i == TPH - 1)
                    last.then_inc(ring_filled, 1)

            with pe.Fori(0, B) as b:
                pe.wait_ge(h_lo, b * 3 + 1)
                for i, name in enumerate(("L0.q", "L0.k")):
                    project(b, name, lambda j, c: wqk0[j][:, i, c, :], h)
                for i in range(2):
                    token_project(b, f"L0.v{i}", h, wv0, i * TPH)
                wait_read(pe, b, "L0.k")
                full_attention(b, "L0")
                group_normed(b, "L1")
                causal_layer(b)
                group_normed(b, "L3")

        @block.scalar
        def _(act):
            A = nc.scalar.activation

            act.wait_ge(weights_in, ALL_LOADED)
            for n, (src, two, idx, _, _) in enumerate(SPLIT):
                act.wait_ge(prep_step, n + 2)
                nc.scalar.copy(part(two, 0, idx), src).then_inc(prep_hi, 1)
            act.wait_ge(prep_done, 3)
            nc.scalar.copy(idle_act[:, :], gamma[:, :]).then_inc(act_read, START)

            def hi(b, name, dst, src=None, bias=0.0, scale=1.0):
                wait_filled(act, b, name)
                A(dst, flat(name) if src is None else src, ACT.Identity, bias=bias,
                  scale=scale).then_inc(hi_ready, 1)

            def values_hi(b, l):
                for i in range(2):
                    hi(b, f"{l}.v{i}", vt[0][:, i * TPH:(i + 1) * TPH, :].rearrange("p t c -> p (t c)"))

            def full_attention(b, l):
                def exp(ti):
                    act.wait_ge(row_max_ready, b * (3 * NT) + LAYER3[l] * NT + ti + 1)
                    if ti >= 2:
                        wait_filled(act, b, f"{l}.t{ti - 2}")
                    A(probs[:, ti % 2, :], flat(f"{l}.s{ti}"), ACT.Exp, bias=neg_max[:, ti:ti + 1],
                      accum_out=row_sum[:, ti:ti + 1]).then_inc(act_read, 1)

                def turned(ti):
                    ts = slice((ti % TPH) * P, (ti % TPH + 1) * P)
                    hi(b, f"{l}.t{ti}", probsT[0][:, ti // TPH, :, ts],
                       slot(f"{l}.t{ti}").rearrange("p b (s n) -> p (b s) n", n=P))

                exp(0)
                exp(1)
                for ti in range(NT):
                    turned(ti)
                    if ti + 2 < NT:
                        exp(ti + 2)

            def group_normed(b, l):
                n = 1 if l == "L1" else 2
                act.wait_ge(gn_coef_ready, b * 2 + n)
                for c in range(CT):
                    last = A(h[0][:, c, :], x[:, c, :], ACT.Identity, scale=gn_sc[:, c:c + 1],
                             bias=gn_nb[:, c:c + 1])
                last.then_inc(h_hi, 1)
                for m in range(CT):
                    hi(b, f"{l}.q{m}", q[0][:, m, :], bias=bqs[l][:, m:m + 1])
                    hi(b, f"{l}.k{m}", k[0][:, m, :], bias=vec(f"{l}_bk", m))
                values_hi(b, l)
                full_attention(b, l)

            def causal_layer(b):
                for hf in range(NB):
                    wait_filled(act, b, f"L2.xt{hf}")
                    nc.scalar.copy(xs[:, hf * TPH:(hf + 1) * TPH, :].rearrange("p t c -> p (t c)"),
                                   flat(f"L2.xt{hf}")).then_inc(act_read, 1)

                def normed_hi(name, hf):
                    hi(b, name, h[0][:, :, hf * HALF:(hf + 1) * HALF], slot(name))

                normed_hi("L2.xn0", 0)
                normed_hi("L2.xn1", 1)
                hi(b, "L2.q0", q2[0][:, 0, :], bias=bq2[:, 0:1])
                hi(b, "L2.kv", ks[0:3 * DH, :], flat("L2.kv")[0:3 * DH, :], bias=bkv2[0:3 * DH, :])
                hi(b, "L2.q1", q2[0][:, 1, :], bias=bq2[:, 1:2])
                for e in schedule:
                    if e[0] == "shift":
                        wait_filled(act, b, event_name(e))
                        nc.scalar.copy(max_rows[:, e[1] % 2, :], slot(event_name(e))[:, 0, :]).then_inc(act_read, 1)
                    elif e[0] == "exp":
                        _, kk, jt, two, step = e
                        ib = blocks[kk][1]
                        n = (ib + 1) * HALF - max(jt * P, ib * HALF)
                        wait_filled(act, b, event_name(e))
                        A(causal_probs(step, two, n), slot(event_name(e))[:, :, 0:n],
                          ACT.Exp).then_inc(act_read, 1)
                for hf in (1, 0):
                    normed_hi(f"L2.ta{hf}", hf)
                for hf in (1, 0):
                    sl = slice(hf * HALF, (hf + 1) * HALF)
                    wait_filled(act, b, f"L2.tg{hf}")
                    for c in range(CT):
                        last = A(gelu[:, c, sl], slot(f"L2.tg{hf}")[:, c, :], ACT.Gelu,
                                 scale=vec("L2_f2_g", c), bias=vec("L2_f2_b", c))
                    last.then_inc(act_read, 1)
                    wait_filled(act, b, f"L2.w2_{hf}")
                    for c in range(CT):
                        last = A(x[:, c, sl], slot(f"L2.w2_{hf}")[:, c, :], ACT.Identity, bias=vec("L2_b2", c))
                    last.then_inc(act_read, 1)

            with act.Fori(0, B) as b:
                act.wait_ge(x_in, b * 16 + 16)
                nc.scalar.copy(h[0][:, :, :], xin[:, :, :]).then_inc(h_hi, 1)
                hi(b, "L0.q", qs0[:, :], bias=bqk0[:, 0:1])
                hi(b, "L0.k", ks0[:, :], bias=bqk0[:, 1:2])
                values_hi(b, "L0")
                full_attention(b, "L0")
                group_normed(b, "L1")
                causal_layer(b)
                group_normed(b, "L3")

        @block.vector
        def _(dve):
            steps = [0]
            v = nc.vector

            def then(b, ins):
                steps[0] += 1
                ins.then_inc(dve_step, 1)
                dve.wait_ge(dve_step, b * DVE_STEPS + steps[0])

            def f32(ap):
                return ap.bitcast(F32)

            dve.wait_ge(weights_in, ALL_LOADED)
            for c in range(CT):
                last = v.tensor_copy(f1b_wide[:, c, :], vec("L2_f1_b", c).broadcast_to([P, P]))
            last.then_inc(prep_step, 1)
            dve.wait_ge(prep_mm, 3)
            for n, (src, two, idx, g, s) in enumerate(SPLIT):
                v.tensor_scalar(src, src, s if g is None else g, None if g is None else s, ALU.mult,
                                ALU.bypass if g is None else ALU.mult).then_inc(prep_step, 1)
            for l, o in (("L1", acc), ("L3", ring[:, 0, :, :])):
                v.tensor_tensor(bvo[l][:, :], o[:, :, C:C + 1].rearrange("p c o -> p (c o)"),
                                vecs[:, VECS.index(f"{l}_bo"), :], ALU.add)
                v.tensor_scalar(bqs[l][:, :], vecs[:, VECS.index(f"{l}_bq"), :], C ** -0.5, None, ALU.mult)
                v.tensor_copy(wvo[l][0][:, :, :], o[:, :, 0:C]).then_inc(prep_done, 1)
            o = ring[:, 1, 0, :]
            v.tensor_scalar(bq2[:, :], o[:, 0:HG], DH ** -0.5, None, ALU.mult)
            v.tensor_copy(bkv2[:, :], o[:, 2:3])
            v.tensor_tensor(rows[:, 2, :], rows[:, 2, :], o[:, C:2 * C], ALU.add)
            bv0 = vecs[:, VECS.index("L0_bv"), :]
            v.tensor_scalar(bv0, bv0, gamma[:, 0:1], None, ALU.mult)
            for n, (src, two, idx, g, s) in enumerate(SPLIT):
                dve.wait_ge(prep_hi, n + 1)
                v.tensor_tensor(part(two, 1, idx), src, f32(part(two, 0, idx)), ALU.subtract)
            dve.wait_ge(prep_done, 2)
            for l, o in (("L1", acc), ("L3", ring[:, 0, :, :])):
                last = v.tensor_tensor(wvo[l][1][:, :, :], o[:, :, 0:C], f32(wvo[l][0][:, :, :]), ALU.subtract)
            last.then_inc(prep_done, 1)
            dve.wait_ge(prep_done, 3)
            v.memset(idle_dve[:, 0:1], 0.0).then_inc(dve_read, START)
            dve.wait_ge(dve_read, START)
            v.memset(idle_dve[:, 0:1], 0.0).then_inc(acc_read, START)
            dve.wait_ge(acc_read, START)

            def lo(b, name, dst, hi, src=None, bias=None, signal=True):
                wait_hi(dve, b, name)
                src = flat(name) if src is None else src
                if bias is None:
                    ins = v.tensor_tensor(dst, src, f32(hi), ALU.subtract)
                else:
                    ins = v.scalar_tensor_tensor(out=dst, in0=src, scalar=bias, in1=f32(hi), op0=ALU.add,
                                                 op1=ALU.subtract)
                if signal:
                    ins.then_inc(dve_read, 1)

            def values_lo(b, l):
                for i in range(2):
                    ap = [s[:, i * TPH:(i + 1) * TPH, :].rearrange("p t c -> p (t c)") for s in vt]
                    lo(b, f"{l}.v{i}", ap[1], ap[0])

            def full_attention(b, l, base, bias, dst):
                first = b * (3 * NT) + LAYER3[l] * NT

                def row_max(ti):
                    wait_filled(dve, b, f"{l}.s{ti}")
                    v.tensor_reduce(neg_max[:, ti:ti + 1], flat(f"{l}.s{ti}"), AX_X, ALU.max,
                                    negate=True).then_inc(row_max_ready, 1)

                def scale(ti):
                    wait_read(dve, b, f"{l}.s{ti}")
                    then(b, v.reciprocal(row_inv[:, ti:ti + 1], row_sum[:, ti:ti + 1]))
                    v.tensor_scalar(probs[:, ti % 2, :], probs[:, ti % 2, :], row_inv[:, ti:ti + 1],
                                    None, ALU.mult).then_inc(probs_scaled, 1)

                def turned(ti):
                    ts = slice((ti % TPH) * P, (ti % TPH + 1) * P)
                    ap = [s[:, ti // TPH, :, ts] for s in probsT]
                    lo(b, f"{l}.t{ti}", ap[1], ap[0], slot(f"{l}.t{ti}").rearrange("p b (s n) -> p (b s) n", n=P))

                def residual(ib, ct):
                    sl = slice(ib * HALF, (ib + 1) * HALF)
                    dve.wait_ge(acc_filled, b * ACCS + acc_no[f"{l}.{ib}{ct}"] + 1)
                    v.scalar_tensor_tensor(out=dst[:, ct, sl], in0=acc[:, ct, :], scalar=bias(ct),
                                           in1=base[:, ct, sl], op0=ALU.add, op1=ALU.add).then_inc(acc_read, 1)
                    if l == "L0":
                        wait_acc_read(dve, b, f"{l}.{ib}{ct}")
                        ins = v.bn_stats(gn_stats[:, ct, ib, :], dst[:, ct, sl])
                        if ib == NB - 1 and ct == CT - 1:
                            then(b, ins)

                row_max(0)
                for ti in range(NT):
                    if ti + 1 < NT:
                        row_max(ti + 1)
                    scale(ti)
                    if ti:
                        turned(ti - 1)
                    if ti == 6:
                        residual(0, 0)
                turned(NT - 1)
                residual(0, 1)
                residual(1, 0)
                residual(1, 1)

            def group_normed(b, l, dst):
                n = 1 if l == "L1" else 2
                r = norm_no[f"{l}.gn"]
                v.memset(idle_dve[:, r:r + 1], 0.0)
                v.bn_aggr(gn_mv[:, 0, :], gn_stats[:, 0, :, :].rearrange("p h s -> p (h s)"))
                then(b, v.bn_aggr(gn_mv[:, 1, :], gn_stats[:, 1, :, :].rearrange("p h s -> p (h s)")))
                mean, var = gn_mv[:, :, 0], gn_mv[:, :, 1]
                then(b, v.tensor_tensor(gn_sq[:, :], mean, mean, ALU.mult))
                v.tensor_copy(gn_in[:, :, 0], mean)
                v.tensor_tensor(gn_in[:, :, 1], gn_sq[:, :], var, ALU.add).then_inc(gn_in_ready, 1)
                wait_filled(dve, b, f"{l}.gn")
                v.tensor_copy(gn_out[:, :, :].rearrange("p c s -> p (c s)"),
                              slot(f"{l}.gn")[:, 0, 0:2 * CT]).then_inc(dve_read, 1)
                wait_read(dve, b, f"{l}.gn")
                gmean, gsq = gn_out[:, :, 0], gn_out[:, :, 1]
                then(b, v.tensor_tensor(gn_sq[:, :], gmean, gmean, ALU.mult))
                v.scalar_tensor_tensor(out=var_eps[:, r, 0:CT], in0=gsq, scalar=EPS_GN, in1=gn_sq[:, :],
                                       op0=ALU.add, op1=ALU.subtract).then_inc(var_ready, 1)
                dve.wait_ge(rstd_ready, b * NORMS + r + 1)
                then(b, v.tensor_tensor(gn_sc[:, :], rstd[:, r, 0:CT], vecs[:, VECS.index(f"{l}_g"), :], ALU.mult))
                then(b, v.tensor_tensor(gn_msc[:, :], gmean, gn_sc[:, :], ALU.mult))
                v.tensor_tensor(gn_nb[:, :], vecs[:, VECS.index(f"{l}_b"), :], gn_msc[:, :],
                                ALU.subtract).then_inc(gn_coef_ready, 1)
                dve.wait_ge(gn_coef_ready, b * 2 + n)
                for c in range(CT):
                    ins = v.tensor_scalar(h_full[:, c, :], x[:, c, :], gn_sc[:, c:c + 1], gn_nb[:, c:c + 1],
                                          ALU.mult, ALU.add)
                then(b, ins)
                dve.wait_ge(h_hi, b * 3 + n + 1)
                for c in range(CT):
                    ins = v.tensor_tensor(h[1][:, c, :], h_full[:, c, :], f32(h[0][:, c, :]), ALU.subtract)
                ins.then_inc(h_lo, 1)
                for m in range(CT):
                    lo(b, f"{l}.q{m}", q[1][:, m, :], q[0][:, m, :], bias=bqs[l][:, m:m + 1])
                    if l == "L1" and m == 0:
                        dve.wait_ge(y_free, b + 1)
                    lo(b, f"{l}.k{m}", k[1][:, m, :], k[0][:, m, :], bias=vec(f"{l}_bk", m))
                values_lo(b, l)
                full_attention(b, l, x, lambda ct: bvo[l][:, ct:ct + 1], dst)

            def layer_norm(b, name, src, dst, hf, signal):
                r = norm_no[name]
                tiles = range(hf * TPH, (hf + 1) * TPH)
                for i, ti in enumerate(tiles):
                    ins = v.bn_stats(ln_stats[:, r, i, :], src[:, ti, :])
                then(b, ins)
                v.memset(idle_dve[:, r:r + 1], 0.0)
                for i in range(TPH):
                    ins = v.bn_aggr(ln_mv[:, r, i, :], ln_stats[:, r, i, :])
                then(b, ins)
                v.tensor_scalar(var_eps[:, r, :], ln_mv[:, r, :, 1], EPS_LN, None, ALU.add).then_inc(var_ready, 1)
                dve.wait_ge(rstd_ready, b * NORMS + r + 1)
                for i, ti in enumerate(tiles):
                    ins = v.tensor_scalar(dst[:, ti, :], src[:, ti, :], ln_mv[:, r, i, 0:1],
                                          rstd[:, r, i:i + 1], ALU.subtract, ALU.mult)
                if signal:
                    ins.then_inc(ln_ready, 1)
                else:
                    then(b, ins)

            def causal_layer(b):
                v.memset(ks[3 * DH:3 * DH + 2, :].bitcast(F32), 1.0).then_inc(one_rows, 1)
                for hf in range(NB):
                    wait_read(dve, b, f"L2.xt{hf}")
                    layer_norm(b, f"L2.ln1.{hf}", xs, an, hf, True)

                def normed_lo(name, hf):
                    ap = [s[:, :, hf * HALF:(hf + 1) * HALF] for s in h]
                    lo(b, name, ap[1], ap[0], slot(name))

                normed_lo("L2.xn0", 0)
                normed_lo("L2.xn1", 1)
                lo(b, "L2.q0", q2[1][:, 0, :], q2[0][:, 0, :], bias=bq2[:, 0:1])
                wait_hi(dve, b, "L2.kv")
                kv = flat("L2.kv")
                v.tensor_scalar(an[3 * DH:P, 0:TPH, :].rearrange("p t c -> p (t c)"), kv[3 * DH:P, :],
                                bkv2[3 * DH:P, :], None, ALU.add)
                lo(b, "L2.kv", ks[DH:2 * DH, :], ks[DH:2 * DH, :], kv[DH:2 * DH, :], bias=bkv2[DH:2 * DH, :])
                lo(b, "L2.q1", q2[1][:, 1, :], q2[0][:, 1, :], bias=bq2[:, 1:2])
                wait_filled(dve, b, "L2.v")
                v.tensor_copy(v2[:, :, :], slot("L2.v").rearrange("p b (s n) -> p (b s) n", n=P)[:, :, 3 * DH:P]
                              ).then_inc(dve_read, 1)

                for e in schedule:
                    if e[0] == "max":
                        _, kk, ti, ch, lo_key, hi_key, two = e
                        n = hi_key - lo_key
                        name = event_name(e)
                        i = ti % TPH
                        cols = cmax[:, kk % 2, i, 2 * two:2 * two + 2]
                        parts = part_max[:, i, :, 2 * two:2 * two + 2]
                        wait_filled(dve, b, name)
                        if hi_key == (ti + 1) * P:
                            d = slot(name)[:, :, n - P:n]
                            then(b, v.tensor_tensor(d, d, causal.unsqueeze(1).broadcast_to([P, 2, P]), ALU.add))
                        v.tensor_reduce(cols if ti < TPH else parts[:, ch, :], slot(name)[:, :, 0:n], AX_X,
                                        ALU.max, negate=True).then_inc(dve_read, 1)
                        if ch == 1:
                            wait_read(dve, b, name)
                            ins = v.tensor_tensor(cols, parts[:, 0, :], parts[:, 1, :], ALU.min)
                            if i == TPH - 1 and two == 1:
                                then(b, ins)
                        if e == last_max[kk]:
                            wait_read(dve, b, name)
                            s = kk % 2
                            then(b, v.tensor_copy(cmax_hi[:, s, :, :], cmax[:, s, :, :]))
                            v.tensor_copy(max_cols[:, s, :, 0:P:DH], f32(cmax_hi[:, s, :, :]))
                            v.tensor_tensor(max_cols[:, s, :, 1:P:DH], cmax[:, s, :, :], f32(cmax_hi[:, s, :, :]),
                                            ALU.subtract).then_inc(max_ready, 1)
                    elif e[0] == "values":
                        _, kk, jt, step = e
                        hg, ib = blocks[kk]
                        if jt == TPH * (ib + 1) - 1:
                            sl = slice(ib * HALF, (ib + 1) * HALF)
                            if kk:
                                dve.wait_ge(out_ready, b * len(blocks) + kk)
                            dve.wait_ge(acc_filled, b * ACCS + acc_no[f"L2.{kk}"] + 1)
                            then(b, v.reciprocal(inv_den[:, :], acc[:, 1, :]))
                            v.tensor_tensor(inv_den[:, :], acc[:, 0, :], inv_den[:, :], ALU.mult).then_inc(acc_read, 1)
                            wait_acc_read(dve, b, f"L2.{kk}")
                            then(b, v.tensor_copy(heads_out[0][:, hg, sl], inv_den[:, :]))
                            v.tensor_tensor(heads_out[1][:, hg, sl], inv_den[:, :], f32(heads_out[0][:, hg, sl]),
                                            ALU.subtract).then_inc(out_ready, 1)

                def row(i):
                    return rows[:, i, :].unsqueeze(1).broadcast_to([P, TPH, C])

                def four(name):
                    return slot(name).rearrange("p b (s c) -> p (b s) c", c=C)

                for hf in (1, 0):
                    ts = slice(hf * TPH, (hf + 1) * TPH)
                    wait_filled(dve, b, f"L2.wo{hf}")
                    v.tensor_tensor(xs[:, ts, :], four(f"L2.wo{hf}"), xs[:, ts, :], ALU.add).then_inc(dve_read, 1)
                    wait_read(dve, b, f"L2.wo{hf}")
                    layer_norm(b, f"L2.ln2.{hf}", xs, xs, hf, False)
                    then(b, v.tensor_tensor(xs[:, ts, :], xs[:, ts, :], row(0), ALU.mult))
                    then(b, v.tensor_tensor(xs[:, ts, :], xs[:, ts, :], row(1), ALU.add))
                    layer_norm(b, f"L2.f1.{hf}", xs, an, hf, True)
                for hf in (1, 0):
                    normed_lo(f"L2.ta{hf}", hf)
                    ts = slice(hf * TPH, (hf + 1) * TPH)
                    wait_filled(dve, b, f"L2.w1_{hf}")
                    v.tensor_tensor(an[:, ts, :], four(f"L2.w1_{hf}"), row(2), ALU.add).then_inc(dve_read, 1)
                    wait_read(dve, b, f"L2.w1_{hf}")
                    layer_norm(b, f"L2.f2.{hf}", an, an, hf, True)
                for n, hf in enumerate((1, 0)):
                    sl = slice(hf * HALF, (hf + 1) * HALF)
                    wait_read(dve, b, f"L2.tg{hf}")
                    then(b, v.tensor_copy(act2[0][:, :, sl], gelu[:, :, sl]))
                    v.tensor_tensor(act2[1][:, :, sl], gelu[:, :, sl], f32(act2[0][:, :, sl]),
                                    ALU.subtract).then_inc(act2_ready, 1)
                for hf in (1, 0):
                    wait_read(dve, b, f"L2.w2_{hf}")
                    for c in range(CT):
                        ins = v.bn_stats(gn_stats[:, c, hf, :], x[:, c, hf * HALF:(hf + 1) * HALF])
                then(b, ins)

            with dve.Fori(0, B) as b:
                steps[0] = 0
                dve.wait_ge(x_in, b * 16 + 16)
                dve.wait_ge(h_hi, b * 3 + 1)
                v.tensor_tensor(h[1][:, :, :], xin[:, :, :], f32(h[0][:, :, :]), ALU.subtract).then_inc(h_lo, 1)
                lo(b, "L0.q", qs0[2 * DH:P, :], qs0[2 * DH:P, :], flat("L0.q")[2 * DH:P, :],
                   bias=bqk0[2 * DH:P, 0:1])
                for g in (1, 3):
                    gs = slice(g * DH, (g + 1) * DH)
                    lo(b, "L0.k", ks0[gs, :], ks0[gs, :], flat("L0.k")[gs, :], bias=bqk0[gs, 1:2], signal=g == 3)
                values_lo(b, "L0")
                full_attention(b, "L0", xin, lambda ct: bv0[:, ct:ct + 1], x)
                group_normed(b, "L1", x)
                causal_layer(b)
                group_normed(b, "L3", y)
            assert steps[0] == DVE_STEPS, steps[0]


def kernel(**inputs):
    import numpy as _np
    import concourse.bacc as _bacc
    from concourse import mybir as _mybir
    from concourse.bass_utils import run_bass_kernel_spmd as _run

    i = {n: _np.asarray(a) for n, a in inputs.items()}
    cols = [i["L0_conv_bv"]] + [i[f"L1_conv_{n}"] for n in ("gn_scale", "gn_bias", "bq", "bk", "bv", "bo")]
    cols += [i[f"L2_conv_{n}"] for n in ("ln1_g", "ln1_b", "ff_ln1_g", "ff_ln1_b", "ff_ln2_g", "ff_ln2_b", "ff_b2")]
    cols += [i[f"L3_conv_{n}"] for n in ("norm_g", "norm_b", "bq", "bk", "bv", "bo")]
    group = C // 32
    channel = _np.arange(P)
    consts = _np.stack([
        _np.eye(P, dtype=_np.float32),
        (channel[:, None] // group == channel[None, :] // group).astype(_np.float32) / _np.float32(group),
        _np.where(channel[None, :] > channel[:, None], _np.float32(-3e38), _np.float32(0)),
    ])
    arrays = {
        "x": i["x"],
        "L0_WqT": i["L0_conv_Wq"].T, "L0_WkT": i["L0_conv_Wk"].T, "L0_WvT": i["L0_conv_Wv"].T,
        "L0_bq": i["L0_conv_bq"].reshape(DH, 1), "L0_bk": i["L0_conv_bk"].reshape(DH, 1),
        "gamma": i["L0_conv_gamma"],
        "vecs": _np.stack(cols).reshape(len(VECS), CT, P).transpose(2, 0, 1),
        "rows": _np.stack([i["L2_conv_ln2_g"], i["L2_conv_ln2_b"], i["L2_conv_ff_b1"]]),
        "consts": consts.transpose(1, 0, 2),
        "L2_wq": i["L2_conv_wq"], "L2_wkv": i["L2_conv_wkv"], "L2_wo": i["L2_conv_wo"],
        "L2_w1": i["L2_conv_ff_w1"], "L2_w2": i["L2_conv_ff_w2"],
    }
    for l in ("L1", "L3"):
        arrays[f"{l}_wqT"] = i[f"{l}_conv_wq"].T
        arrays[f"{l}_wkT"] = i[f"{l}_conv_wk"].T
        arrays[f"{l}_wv"] = i[f"{l}_conv_wv"]
        arrays[f"{l}_woT"] = i[f"{l}_conv_wo"].T
    arrays = {f"{n}_dram": _np.ascontiguousarray(a) for n, a in arrays.items()}
    nc = _bacc.Bacc("TRN2", target_bir_lowering=False, num_devices=1)
    tensors = {n[:-5]: nc.dram_tensor(n, a.shape, _mybir.dt.from_np(a.dtype), kind="ExternalInput").ap()
               for n, a in arrays.items()}
    tensors["out"] = nc.dram_tensor("out_dram", (B, C, 32, 32), _mybir.dt.float32, kind="ExternalOutput").ap()
    build(nc, tensors)
    r = _run(nc, [arrays], core_ids=[0])
    return r.results[0]["out_dram"]
```

```python
from contextlib import ExitStack

import concourse.bass as bass
from concourse import mybir

F32 = mybir.dt.float32
F32R = mybir.dt.float32r
BF16 = mybir.dt.bfloat16
ALU = mybir.AluOpType
ACT = mybir.ActivationFunctionType
AX_X = mybir.AxisListType.X

P = 128
B, C, N = 4, 256, 1024
CT = C // P
NT = N // P
HALF = 512
NB = N // HALF
TPH = HALF // P
HEADS, DH = 8, 32
HG = 2
EPS_GN, EPS_LN = 1e-6, 1e-5
SLOTS = 4
ACC = 3

VECS = ["L0_bv", "L1_g", "L1_b", "L1_bq", "L1_bk", "L1_bv", "L1_bo", "L2_ln1_g", "L2_ln1_b",
        "L2_f1_g", "L2_f1_b", "L2_f2_g", "L2_f2_b", "L2_b2", "L3_g", "L3_b", "L3_bq", "L3_bk",
        "L3_bv", "L3_bo"]
ROWS = ["ln2_g", "ln2_b", "ff_b1"]

DVE_STEPS = 101


def causal_blocks():
    return [(0, 0), (1, 0), (0, 1), (1, 1)]


PARTS = [(0, 4), (4, 2), (6, 2)]
FEED_FORWARD = ("wo", "ln2b", "f1b", "ta", "w1", "f2b", "tg", "w2")
FILLS = ("xt", "xn", "q", "kv", "vt", "wo", "ta", "w1", "tg", "w2")
NORM_PIECES = 6


def attention_order(layer):
    if layer == "L0":
        out = [("v", 0), ("s", 0), ("s", 1), ("s", 2), ("v", 1)]
    else:
        out = [("q", 1), ("s", 0), ("s", 1), ("v", 0), ("s", 2), ("v", 1)]
    for i in range(NT):
        out.append(("t", i))
        if i + 3 < NT:
            out.append(("s", i + 3))
        if i >= TPH:
            out.append(("o", 0, i - TPH))
    last = [("o", 1, i) for i in range(TPH)]
    if layer == "L1":
        last = [last[0], ("xt", 0), last[1], last[2], ("xn", 0), last[3]]
    return out + last


def causal_schedule():
    blocks = causal_blocks()

    def max_events(k):
        hg, ib = blocks[k]
        out = []
        for t in range(TPH * ib, TPH * (ib + 1)):
            end = (t + 1) * P
            for ch, (lo, hi) in enumerate([(0, end)] if end <= HALF else [(0, HALF), (HALF, end)]):
                out += [("max", k, t, ch, lo, hi, pair) for pair in range(2)]
        return out

    first = max_events(0)
    events = [("q", 0), ("xt", 1), ("kv", 0), ("vt", 0), ("xn", 1)] + first[:4]
    events += [("q", 1), ("kv", 1)] + first[4:] + [("shift", 0), ("vt", 1)]
    pending = None
    step = 0
    ahead = [max_events(k) for k in range(len(blocks))]
    fill = [
        ahead[1][4:] + [("shift", 1)] + ahead[2][:6],
        merged(norm(0), ahead[2][6:]) + [("shift", 2)] + ahead[3][:3],
        merged(norm(1), ahead[3][3:]) + [("shift", 3), ("wo", 0)],
        [("ln2b", 0)] + norm(2) + [("f1b", 0), ("ta", 0), ("w1", 0), ("f2b", 0), ("tg", 0), ("w2", 0)],
    ]
    events += ahead[1][:4]
    for k, (hg, ib) in enumerate(blocks):
        base = []
        for jt in range(TPH * (ib + 1)):
            base += [("exp", k, jt, pair, step) for pair in range(2)]
            if pending:
                base.append(pending)
            pending = ("values", k, jt, step)
            step += 1
        start = 2 if k else 0
        done = 0
        for i, e in enumerate(base):
            events.append(e)
            upto = min(len(fill[k]), -(-len(fill[k]) * max(0, i + 1 - start) // (len(base) - start - 2)))
            events += fill[k][done:upto]
            done = upto
    return events + [pending] + norm(len(blocks) - 1) + [(e, part) for e in FEED_FORWARD for part in (1, 2)]


def norm(k):
    return [("norm", k, i) for i in range(NORM_PIECES)]


def merged(a, b):
    return [x for _, _, x in sorted([((i + 0.5) / len(a), 0, x) for i, x in enumerate(a)]
                                    + [((i + 0.5) / len(b), 1, x) for i, x in enumerate(b)])]


def event_name(e):
    if len(e) == 2:
        return f"L2.{e[0]}{e[1]}"
    if e[0] == "values":
        return f"L2.o{e[1]}"
    return "L2." + ".".join(map(str, e[:4] + e[-1:]))


def ring_units():
    units = []
    last = [-1] * SLOTS

    def add(name, eng, held):
        s = min((s for s in range(SLOTS) if s != ACC or not held), key=lambda s: last[s])
        last[s] = len(units)
        units.append((name, eng, s, (0, 1)))

    def accumulated(name, eng, banks):
        last[ACC] = len(units)
        units.append((name, eng, ACC, banks))

    def attention(l):
        held = False
        for e in attention_order(l):
            held = held or e == ("s", NT - 1)
            if e[0] == "o":
                ct, j0 = divmod(e[2] * TPH, NT)
                if j0 + TPH == NT:
                    accumulated(f"{l}.o{e[1]}{ct}", "dve", (ct,))
            elif e[0] in ("xt", "xn"):
                add(event_name(e), "act" if e[0] == "xt" else "dve", held)
            else:
                add(f"{l}.{e[0]}{e[1]}", "act" if e[0] == "s" else "dve", held)

    add("L0.q", "dve", False)
    add("L0.k", "dve", False)
    attention("L0")
    for l in ("L1", "L3"):
        if l == "L3":
            held = False
            for e in causal_schedule():
                if e[0] == "norm" or len(e) == 2 and e[0] not in FILLS + ("shift",):
                    continue
                if e[0] == "values":
                    held = True
                    if e[2] == TPH * (causal_blocks()[e[1]][1] + 1) - 1:
                        accumulated(event_name(e), "act", (0, 1))
                        held = e[1] + 1 < len(causal_blocks())
                else:
                    add(event_name(e), "act" if e[0] in ("xt", "shift", "exp", "tg", "w2") else "dve", held)
        add(f"{l}.gn", "dve", False)
        for u in ("q0", "k0", "k1"):
            add(f"{l}.{u}", "dve", False)
        attention(l)
    return units


def split_units(units):
    kinds = ("q", "k", "v", "t", "xn", "kv", "ta")
    return [u[0] for u in units if u[0].split(".")[1].rstrip("0123456789") in kinds]


def build(nc, t):
    units = ring_units()
    number = {u[0]: i for i, u in enumerate(units)}
    reader = {u[0]: u[1] for u in units}
    where = {u[0]: u[2:] for u in units}
    U = len(units)
    rank, total = {}, {"act": 0, "dve": 0}
    for name, eng, _, _ in units:
        total[eng] += 1
        rank[name] = total[eng]
    halves = split_units(units)
    half_no = {name: i for i, name in enumerate(halves)}
    SPLITS = len(halves)
    schedule = causal_schedule()
    blocks = causal_blocks()
    norms = ["L1.gn", "L2.ln1.0", "L2.ln1.1"]
    for e in schedule:
        if e[0] in ("wo", "ln2b", "w1"):
            norms.append("L2.%s.%d" % ({"wo": "ln2", "ln2b": "f1", "w1": "f2"}[e[0]], e[1]))
    norms.append("L3.gn")
    H_PARTS = 5
    ready = [("xn", 0), ("xn", 1)] + [e for e in schedule if e[0] in ("ta", "tg")]
    norm_no = {name: i for i, name in enumerate(norms)}
    NORMS = len(norms)
    diagonal = [e for e in schedule if e[0] == "exp" and e[2] >= TPH * blocks[e[1]][1]]
    DIAG = len(diagonal)
    last_max = {e[1]: e for e in schedule if e[0] == "max"}
    first_max = {ib: next(e for e in schedule if e[0] == "max" and blocks[e[1]][1] == ib) for ib in range(NB)}
    diag_no = {event_name(e): i for i, e in enumerate(diagonal)}

    with ExitStack() as ctx:
        def sem(name):
            return ctx.enter_context(nc.semaphore(name))

        top = [(nc.sbuf_base + 31) // 32 * 32]

        def region(kib):
            at = top[0]
            top[0] += kib * 1024
            return at

        def place(name, shape, at, dtype=F32):
            size = 2 if dtype == BF16 else 4
            for d in shape[1:]:
                size *= d
            return nc.alloc_sbuf_tensor_at(name, shape, dtype, offset=at), at + size

        def shared(name, shape, at, dtype=F32):
            return place(name, shape, at, dtype)[0]

        def sb(name, shape, dtype=F32):
            tensor, end = place(name, shape, top[0], dtype)
            top[0] = (end + 31) // 32 * 32
            return tensor

        def pair(name, shape, at=None):
            size = 4
            for d in shape[1:]:
                size *= d
            if at is None:
                return sb(f"{name}_hi", shape, F32R), sb(f"{name}_lo", shape, F32R)
            return shared(f"{name}_hi", shape, at, F32R), shared(f"{name}_lo", shape, at + size, F32R)

        KIB = 1024
        r_xin, r_x, r_q, r_k, r_v = region(8), region(8), region(16), region(16), region(16)
        r_p, r_t, r_s = region(8), region(64), region(8)
        xin = shared("xin", [P, CT, N], r_xin)
        x = shared("x", [P, CT, N], r_x)
        h = pair("h", [P, CT, N], r_t)
        q, k = pair("q", [P, CT, N], r_q), pair("k", [P, CT, N], r_k)
        qs0 = shared("qs0", [P, N], r_q, F32R)
        ks0 = shared("ks0", [P, N], r_k, F32R)
        vt = pair("vt", [P, NT, C], r_v)
        probs = shared("probs", [P, 2, N], r_p)
        probsT = pair("probsT", [P, NB, NT, HALF], r_t)
        h_full = shared("h_full", [P, CT, N], r_p)
        y = shared("y", [P, CT, N], r_k + 8 * KIB)
        q2 = pair("q2", [P, HG, N], r_q)
        ks = shared("ks", [P, N], r_k, F32R)
        max_rows = shared("max_rows", [P, 2, HALF], r_k + 4 * KIB, F32R)
        max_cols = shared("max_cols", [P, 2, TPH, P], r_k + 8 * KIB)
        sums = shared("sums", [P, 2, HALF], r_k + 12 * KIB)
        heads_out = pair("heads_out", [P, HG, N], r_v)
        cprobs = shared("cprobs", [P, 4, 4, HALF], r_t)
        qs = shared("qs", [P, HEADS, N], r_t + 32 * KIB, F32R)
        an = shared("an", [P, NT, C], r_p)
        xs = shared("xs", [P, NT, C], r_s)
        gelu = x
        hn = pair("hn", [P, CT, HALF], r_q)
        act2 = pair("act2", [P, CT, HALF], r_q + 8 * KIB)

        raw_at = [r_t]

        def raw(name, shape):
            tensor, raw_at[0] = place(name, shape, raw_at[0])
            return tensor

        raw_qk0 = raw("raw_qk0", [P, 2, CT, P])
        raw_v0 = raw("raw_v0", [P, CT, C])
        raws = {}
        for l in ("L1", "L3"):
            for w in ("wqT", "wkT", "wv", "woT"):
                raws[l, w] = raw(f"raw_{l}_{w}", [P, CT, C])
        raw_q2, raw_kv2 = raw("raw_q2", [P, CT, C]), raw("raw_kv2", [P, CT, P])
        raw_o2, raw_w1, raw_w2 = raw("raw_o2", [P, HG, C]), raw("raw_w1", [P, CT, C]), raw("raw_w2", [P, CT, C])
        f1b_wide = raw("f1b_wide", [P, CT, P])

        wqk0, wv0 = pair("wqk0", [P, 2, CT, P]), pair("wv0", [P, CT, C])
        wq, wk, wvo, bqs, bvo = {}, {}, {}, {}, {}
        for l in ("L1", "L3"):
            wq[l], wk[l] = pair(f"{l}_wq", [P, CT, C]), pair(f"{l}_wk", [P, CT, C])
            wvo[l] = pair(f"{l}_wvo", [P, CT, C])
            bqs[l] = sb(f"{l}_bqs", [P, CT])
            bvo[l] = sb(f"{l}_bvo", [P, CT])
        wq2, wkv2 = pair("wq2", [P, CT, C]), pair("wkv2", [P, CT, P])
        wo2, ffw1, ffw2 = pair("wo2", [P, HG, C]), pair("ffw1", [P, CT, C]), pair("ffw2", [P, CT, C])
        bq2, bkv2 = sb("bq2", [P, HG]), sb("bkv2", [P, 1])
        bqk0 = sb("bqk0", [P, 2])
        gamma = sb("gamma", [P, 1])
        ln1_scaled = sb("ln1_scaled", [P, CT])
        vecs = sb("vecs", [P, len(VECS), CT])
        rows = sb("rows", [P, len(ROWS), C])
        consts = sb("consts", [P, 3, P])
        ones = sb("ones", [P, DH])
        half_neg = sb("half_neg", [P, 4])
        mask = sb("mask", [P, 2, P], BF16)
        ident, group_mean, causal = consts[:, 0, :], consts[:, 1, :], consts[:, 2, :]

        v2 = sb("v2", [P, NT, DH])
        neg_max, row_sum, row_inv = sb("neg_max", [P, NT]), sb("row_sum", [P, NT]), sb("row_inv", [P, NT])
        gn_stats = sb("gn_stats", [P, CT, 2 * NB, 6])
        gn_mv, gn_in, gn_out = sb("gn_mv", [P, CT, 2]), sb("gn_in", [P, CT, 2]), sb("gn_out", [P, CT, 2])
        gn_sq, gn_sc, gn_msc, gn_nb = (sb(f"gn_{s}", [P, CT]) for s in ("sq", "sc", "msc", "nb"))
        var_eps, rstd = sb("var_eps", [P, NORMS, 4]), sb("rstd", [P, NORMS, 4])
        ln_stats, ln_mv = sb("ln_stats", [P, NORMS, TPH, 6]), sb("ln_mv", [P, NORMS, TPH, 2])
        part_max = sb("part_max", [P, TPH, 2, 4])
        cmax = sb("cmax", [P, 2, TPH, 4])
        cmax_hi = sb("cmax_hi", [P, 2, TPH, 4], F32R)
        idle_act = sb("idle_act", [P, 1])
        idle_pool, idle_dve = sb("idle_pool", [P, DIAG]), sb("idle_dve", [P, NORMS])
        assert top[0] <= nc.sbuf_usable_end, (top[0], nc.sbuf_usable_end)

        def causal_probs(step, two, n):
            return cprobs[:, step % 4, 2 * two:2 * two + 2, 0:n]

        ring = ctx.enter_context(nc.psum_tensor("ring", [P, SLOTS, 2, HALF], F32))
        acc = ring[:, ACC, :, :]

        weights_in = {l: sem(f"weights_in_{l}") for l in ("L0", "L1", "L2", "L3")}
        x_in = sem("x_in")
        y_out = sem("y_out")
        stack_in = [sem(f"stack_in{i}") for i in range(NB)]
        shift_in = sem("shift_in")
        y_free = sem("y_free")
        ring_filled = sem("ring_filled")
        hi_ready = sem("hi_ready")
        act_read = sem("act_read")
        dve_read = sem("dve_read")
        row_max_ready = sem("row_max_ready")
        probs_scaled = sem("probs_scaled")
        gn_in_ready = sem("gn_in_ready")
        gn_coef_ready = sem("gn_coef_ready")
        h_hi, h_lo = sem("h_hi"), sem("h_lo")
        gelu_ready = sem("gelu_ready")
        act2_ready = sem("act2_ready")
        out_ready = sem("out_ready")
        var_ready = sem("var_ready")
        rstd_ready = sem("rstd_ready")
        ln_ready = sem("ln_ready")
        max_ready = sem("max_ready")
        one_rows = sem("one_rows")
        diag_masked = sem("diag_masked")
        dve_step = sem("dve_step")
        prep_mm = sem("prep_mm")
        prep_hi = sem("prep_hi")
        prep_vecs = sem("prep_vecs")
        prep_done = sem("prep_done")
        setup = sem("setup")

        LAYER3 = {"L0": 0, "L1": 1, "L3": 2}

        def slot(name):
            return ring[:, where[name][0], :, :]

        def flat(name):
            return slot(name).rearrange("p b n -> p (b n)")

        def wait_read(eng, b, name):
            e = reader[name]
            eng.wait_ge(act_read if e == "act" else dve_read, (b + 1) * total[e] + rank[name])

        def wait_filled(eng, b, name):
            eng.wait_ge(ring_filled, b * U + (number[name] + 1))

        def wait_hi(eng, b, name):
            eng.wait_ge(hi_ready, b * SPLITS + (half_no[name] + 1))

        def vec(name, ct):
            return vecs[:, VECS.index(name), ct:ct + 1]

        LOADS = {"L0": [
            (vecs[:, :, :], t["vecs"]),
            (gamma[:, :], t["gamma"].partition_broadcast(P)),
            (raw_v0[:, :, :], t["L0_WvT"].rearrange("(c p) o -> p c o", p=P)),
            (consts[:, :, :], t["consts"]),
        ], "L1": [], "L2": [], "L3": []}
        LOADS["L0"].append((bqk0[:, :], t["L0_bqk"]))
        for i in range(2):
            LOADS["L0"].append((raw_qk0[:, i, :, :], t["L0_WqkT"][i].rearrange("(c p) o -> p c o", p=P)))
        LOADS["L2"].append((raw_kv2[:, :, :], t["L2_wkv"].rearrange("(c p) o -> p c o", p=P)))
        for l in ("L1", "L3"):
            for w in ("wv", "woT", "wqT", "wkT"):
                LOADS[l].append((raws[l, w][:, :, :], t[f"{l}_{w}"].rearrange("(c p) o -> p c o", p=P)))
        for dst, w in ((raw_q2, "wq"), (raw_w1, "w1"), (raw_o2, "wo"), (raw_w2, "w2")):
            LOADS["L2"].append((dst[:, :, :], t[f"L2_{w}"].rearrange("(c p) o -> p c o", p=P)))
        LOADS["L2"].append((rows[:, :, :], t["rows"].partition_broadcast(P)))

        def wait_loaded(eng, group):
            eng.wait_ge(weights_in[group], 16 * len(LOADS[group]))

        SPLIT = {"L0": [(raw_qk0[:, i, c, :], wqk0, (i, c), 1.0)
                        for i in range(2) for c in range(CT)] + [(raw_v0[:, c, :], wv0, (c,), gamma[:, 0:1])
                                                                  for c in range(CT)], "L2": []}
        for c in range(CT):
            SPLIT["L2"] += [(raw_q2[:, c, :], wq2, (c,), ln1_scaled[:, c:c + 1]),
                            (raw_kv2[:, c, :], wkv2, (c,), vec("L2_ln1_g", c)),
                            (raw_o2[:, c, :], wo2, (c,), 1.0),
                            (raw_w1[:, c, :], ffw1, (c,), vec("L2_f1_g", c)),
                            (raw_w2[:, c, :], ffw2, (c,), 1.0)]
        for l in ("L1", "L3"):
            SPLIT[l] = [(raws[l, "wqT"][:, c, :], wq[l], (c,), C ** -0.5) for c in range(CT)]
            SPLIT[l] += [(raws[l, "wkT"][:, c, :], wk[l], (c,), 1.0) for c in range(CT)]

        def part(two, which, idx):
            ap = two[which]
            return ap[:, idx[0], idx[1], :] if len(idx) == 2 else ap[:, idx[0], :]

        SPLIT_ORDER = ("L0", "L1", "L2", "L3")
        OUTPUT_PRODUCT = {"L1": (1, ACC), "L3": (3, 0)}

        block = ctx.enter_context(nc.Block())

        @block.sync
        def _(sp):
            x_dram = t["x"].rearrange("b (c p) h w -> b p c (h w)", p=P)
            y_dram = t["out"].rearrange("b (c p) h w -> b p c (h w)", p=P)
            sp.dma_start(xin[:, :, :], x_dram[0]).then_inc(x_in, 16)
            for group, loads in LOADS.items():
                for dst, src in loads:
                    sp.dma_start(dst, src).then_inc(weights_in[group], 16)
            sp.sem_inc(y_free, 1)

            def moves(b):
                for ib in range(NB):
                    sl = slice(ib * HALF, (ib + 1) * HALF)
                    wait_read(sp, b, f"L2.q{ib}")
                    for a in range(4):
                        for g, src in enumerate((q2[0], q2[0], q2[1])):
                            sp.dma_start(qs[DH * g:DH * (g + 1), a::4, sl].bitcast(F32),
                                         src[DH * a:DH * (a + 1), :, sl].bitcast(F32)).then_inc(stack_in[ib], 16)
                for kk, (hg, ib) in enumerate(blocks):
                    wait_read(sp, b, event_name(("shift", kk)))
                    for a in range(4):
                        sp.dma_start(qs[3 * DH:3 * DH + 2, 4 * hg + a, ib * HALF:(ib + 1) * HALF].bitcast(F32),
                                     max_rows[DH * a:DH * a + 2, kk % 2, :].bitcast(F32)).then_inc(shift_in, 16)
                for ib in range(NB):
                    wait_read(sp, b, f"L3.o{ib}{CT - 1}")
                    sl = slice(ib * HALF, (ib + 1) * HALF)
                    sp.dma_start(y_dram[b][:, :, sl], y[:, :, sl]).then_inc(y_out, 16)
                sp.wait_ge(y_out, b * (16 * NB) + 16 * NB)
                sp.sem_inc(y_free, 1)

            with sp.Fori(0, B - 1) as b:
                wait_read(sp, b, f"L0.o{NB - 1}{CT - 1}")
                sp.dma_start(xin[:, :, :], x_dram[b + 1]).then_inc(x_in, 16)
                moves(b)
            sp.sem_inc(x_in, 16)
            moves(B - 1)

        @block.gpsimd
        def _(pool):
            pool.memset(ones[:, :], 1.0).then_inc(setup, 1)
            pool.memset(half_neg[:, :], -0.5).then_inc(setup, 1)
            pool.wait_ge(setup, 2)

            def root(b, name):
                n = norm_no[name]
                if name.endswith("gn"):
                    w = CT
                else:
                    w = TPH if name.startswith("L2.ln1") else PARTS[int(name[-1])][1]
                pool.wait_ge(var_ready, b * NORMS + (n + 1))
                pool.tensor_tensor(rstd[:, n, 0:w], var_eps[:, n, 0:w], half_neg[:, 0:w],
                                   ALU.pow).then_inc(rstd_ready, 1)

            with pool.Fori(0, B) as b:
                for name in norms[:3]:
                    root(b, name)
                for e in schedule:
                    if e[0] in ("wo", "ln2b", "w1"):
                        root(b, "L2.%s.%d" % ({"wo": "ln2", "ln2b": "f1", "w1": "f2"}[e[0]], e[1]))
                    elif e in diagonal:
                        i = diag_no[event_name(e)]
                        wait_read(pool, b, event_name(e))
                        d = causal_probs(e[4], e[3], P)
                        pool.tensor_tensor(idle_pool[:, i:i + 1], half_neg[:, 0:1], half_neg[:, 0:1], ALU.mult)
                        pool.affine_select(out=d, in_=d, pattern=[[0, 2], [1, P]], compare_op=ALU.is_ge,
                                           fill=0.0, base=0, channel_multiplier=-1).then_inc(diag_masked, 1)
                root(b, norms[-1])

        @block.tensor
        def _(pe):
            mm = nc.tensor.matmul
            PASSES = ((0, 0), (0, 1), (1, 0))

            def open_unit(b, name):
                s, banks = where[name]
                before = {}
                for bank in banks:
                    same = [i for i, u in enumerate(units) if u[2] == s and bank in u[3]]
                    earlier = [i for i in same if i < number[name]]
                    i, back = (earlier[-1], 0) if earlier else (same[-1], 1)
                    key = (units[i][1], back)
                    before[key] = max(before.get(key, i), i)
                for (_, back), i in before.items():
                    wait_read(pe, b - back if back else b, units[i][0])
                return slot(name)

            def product(out, terms, first=True, last=True):
                every = [(w[i], m[j]) for w, m in terms for i, j in PASSES]
                for n, (w, m) in enumerate(every):
                    ins = mm(out, w, m, start=first and n == 0, stop=last and n == len(every) - 1)
                return ins

            def output_products(l, out):
                wait_loaded(pe, l)
                for ci in range(CT):
                    for m in range(CT):
                        mm(out[:, ci, 0:C], raws[l, "wv"][:, m, ci * P:(ci + 1) * P], raws[l, "woT"][:, m, :],
                           start=m == 0, stop=m == CT - 1)
                for co in range(CT):
                    for m in range(CT):
                        last = mm(out[:, co, C:C + 1], raws[l, "woT"][:, m, co * P:(co + 1) * P],
                                  vec(f"{l}_bv", m), start=m == 0, stop=m == CT - 1)
                last.then_inc(prep_mm, 1)

            wait_loaded(pe, "L0")
            output_products("L1", acc)
            wait_loaded(pe, "L2")
            out = ring[:, 1, 0, :]
            for hg in range(HG):
                for c in range(CT):
                    mm(out[:, hg:hg + 1], raw_q2[:, c, hg * P:(hg + 1) * P], vec("L2_ln1_b", c),
                       start=c == 0, stop=c == CT - 1)
            for c in range(CT):
                mm(out[:, 2:3], raw_kv2[:, c, :], vec("L2_ln1_b", c),
                   start=c == 0, stop=c == CT - 1)
            pe.wait_ge(prep_vecs, 1)
            for c in range(CT):
                last = mm(out[:, C:2 * C], f1b_wide[:, c, :], raw_w1[:, c, :], start=c == 0, stop=c == CT - 1)
            last.then_inc(prep_mm, 1)
            output_products("L3", ring[:, 0, :, :])
            pe.wait_ge(setup, 2)

            def project(b, name, weights, src, sl):
                o = open_unit(b, name)
                for bank, w in enumerate(weights):
                    last = product(o[:, bank, :], [([w(i, c) for i in (0, 1)], [s[:, c, sl] for s in src])
                                                   for c in range(CT)])
                last.then_inc(ring_filled, 1)

            def token_project(b, name, src, w, t0, n=TPH):
                o = open_unit(b, name).rearrange("p b (s c) -> p (b s) c", c=C)
                for i in range(n):
                    sl = slice((t0 + i) * P, (t0 + i + 1) * P)
                    last = product(o[:, i, :], [([s[:, c, sl] for s in src], [u[:, c, :] for u in w])
                                                for c in range(CT)])
                last.then_inc(ring_filled, 1)

            def full_attention(b, l):
                def scores(ti):
                    o = open_unit(b, f"{l}.s{ti}")
                    ts = slice(ti * P, (ti + 1) * P)
                    for hf in range(NB):
                        keys = slice(hf * HALF, (hf + 1) * HALF)
                        if l == "L0":
                            last = mm(o[:, hf, :], qs0[0:3 * DH, ts], ks0[0:3 * DH, keys], start=True, stop=True)
                        else:
                            last = product(o[:, hf, :], [([s[:, c, ts] for s in q], [s[:, c, keys] for s in k])
                                                         for c in range(CT)])
                    last.then_inc(ring_filled, 1)

                def turn(ti):
                    o = open_unit(b, f"{l}.t{ti}").rearrange("p b (s n) -> p (b s) n", n=P)
                    pe.wait_ge(probs_scaled, b * (3 * NT) + LAYER3[l] * NT + ti + 1)
                    for j in range(NT):
                        last = nc.tensor.transpose(o[:, j, :], probs[:, ti % 2, j * P:(j + 1) * P], ident)
                    last.then_inc(ring_filled, 1)

                def values(ib, quarter):
                    ct, j0 = divmod(quarter * TPH, NT)
                    if j0 == 0:
                        open_unit(b, f"{l}.o{ib}{ct}")
                    last = product(acc[:, ct, :], [([s[:, j, ct * P:(ct + 1) * P] for s in vt],
                                                    [s[:, ib, j, :] for s in probsT])
                                                   for j in range(j0, j0 + TPH)],
                                   first=j0 == 0, last=j0 + TPH == NT)
                    if j0 + TPH == NT:
                        last.then_inc(ring_filled, 1)

                for e in attention_order(l):
                    if e[0] == "s":
                        if e[1] == 0:
                            wait_read(pe, b, "L0.k" if l == "L0" else f"{l}.k1")
                        if e[1] == TPH and l != "L0":
                            wait_read(pe, b, f"{l}.q1")
                        scores(e[1])
                    elif e[0] == "q":
                        project(b, f"{l}.q1", both(wq[l]), h, token_half(1))
                    elif e[0] == "v":
                        token_project(b, f"{l}.v{e[1]}", h, wv0 if l == "L0" else wvo[l], e[1] * TPH)
                    elif e[0] == "t":
                        turn(e[1])
                    elif e[0] == "o":
                        _, ib, quarter = e
                        if quarter == 0:
                            wait_read(pe, b, f"{l}.t{TPH * (ib + 1) - 1}")
                        values(ib, quarter)
                    else:
                        stage(b, e)

            def token_half(hf):
                return slice(hf * HALF, (hf + 1) * HALF)

            def both(w):
                return [lambda i, c, ms=slice(m * P, (m + 1) * P): w[i][:, c, ms] for m in range(CT)]

            def group_normed(b, l):
                n = 1 if l == "L1" else 2
                pe.wait_ge(gn_in_ready, b * 2 + n)
                o = open_unit(b, f"{l}.gn")
                mm(o[:, 0, 0:2 * CT], group_mean, gn_in[:, :, :].rearrange("p c s -> p (c s)"),
                   start=True, stop=True).then_inc(ring_filled, 1)
                pe.wait_ge(h_lo, b * H_PARTS + 2 * n)
                project(b, f"{l}.q0", both(wq[l]), h, token_half(0))
                project(b, f"{l}.k0", both(wk[l]), h, token_half(0))
                pe.wait_ge(h_lo, b * H_PARTS + 2 * n + 1)
                project(b, f"{l}.k1", both(wk[l]), h, token_half(1))
                full_attention(b, l)

            def stage(b, e):
                kind, hf = e
                if kind not in FILLS:
                    return
                name = event_name(e)
                sl = token_half(hf)
                t0, n = PARTS[hf]
                at = (t0 % TPH) * P
                if kind == "xt":
                    wait_read(pe, b, f"L1.o{hf}{CT - 1}")
                    o = open_unit(b, name).rearrange("p b (s c n) -> p (b s) c n", c=CT, n=P)
                    for i in range(TPH):
                        for c in range(CT):
                            last = nc.tensor.transpose(o[:, i, c, :], x[:, c, hf * HALF + i * P:hf * HALF + (i + 1) * P],
                                                       ident)
                    last.then_inc(ring_filled, 1)
                elif kind in ("xn", "ta", "tg"):
                    if kind == "xn":
                        t0, n = hf * TPH, TPH
                    pe.wait_ge(ln_ready, b * len(ready) + ready.index(e) + 1)
                    o = open_unit(b, name)
                    for i in range(n):
                        for c in range(CT):
                            last = nc.tensor.transpose(o[:, c, i * P:(i + 1) * P], an[:, t0 + i, c * P:(c + 1) * P],
                                                       ident)
                    last.then_inc(ring_filled, 1)
                elif kind == "q":
                    wait_read(pe, b, f"L2.xn{hf}")
                    project(b, name, both(wq2), h, sl)
                elif kind == "kv":
                    project(b, name, [lambda i, c: wkv2[i][:, c, :]], h, sl)
                elif kind == "vt":
                    wait_read(pe, b, f"L2.kv{hf}")
                    o = open_unit(b, name)
                    for i in range(TPH):
                        last = nc.tensor.transpose(o[:, 0, i * P:(i + 1) * P],
                                                   an[:, 2 * hf + i // 2, (i % 2) * P:(i % 2 + 1) * P], ident)
                    last.then_inc(ring_filled, 1)
                elif kind == "wo":
                    pe.wait_ge(out_ready, b * (2 * len(blocks)) + {0: 4, 1: 7, 2: 8}[hf])
                    token_project(b, name, heads_out, wo2, t0, n)
                elif kind == "w1":
                    wait_read(pe, b, f"L2.ta{hf}")
                    token_project(b, name, hn, ffw1, t0 % TPH, n)
                elif kind == "w2":
                    o = open_unit(b, name)
                    for co in range(CT):
                        for i in range(n):
                            mm(o[:, co, i * P:(i + 1) * P], xs[:, t0 + i, co * P:(co + 1) * P], ident,
                               start=i == 0, stop=False)
                    pe.wait_ge(act2_ready, b * len(PARTS) + hf + 1)
                    for co in range(CT):
                        cs = slice(co * P, (co + 1) * P)
                        last = product(o[:, co, 0:n * P], [([w[:, c, cs] for w in ffw2],
                                                            [a[:, c, at:at + n * P] for a in act2])
                                                           for c in range(CT)], first=False)
                    last.then_inc(ring_filled, 1)

            def causal_layer(b):
                for e in schedule:
                    if len(e) == 2 and e[0] != "shift":
                        stage(b, e)
                        continue
                    if e[0] == "norm":
                        continue
                    kk = e[1]
                    hg, ib = blocks[kk]
                    if e[0] == "max":
                        _, _, ti, _, lo, hi, two = e
                        if e == first_max[ib]:
                            wait_read(pe, b, f"L2.kv{ib}")
                            pe.wait_ge(stack_in[ib], b * (16 * 12) + 16 * 12)
                        o = open_unit(b, event_name(e))
                        diag = hi == (ti + 1) * P
                        for i in range(2):
                            last = mm(o[:, i, 0:hi - lo], qs[0:3 * DH, 4 * hg + 2 * two + i, ti * P:(ti + 1) * P],
                                      ks[0:3 * DH, lo:hi], start=True, stop=not diag)
                            if diag:
                                last = mm(o[:, i, hi - lo - P:hi - lo], mask[:, 0, :], mask[:, 1, :],
                                          start=False, stop=True)
                        last.then_inc(ring_filled, 1)
                    elif e[0] == "shift":
                        pe.wait_ge(max_ready, b * len(blocks) + kk + 1)
                        o = open_unit(b, event_name(e))
                        for i in range(TPH):
                            last = nc.tensor.transpose(o[:, 0, i * P:(i + 1) * P], max_cols[:, kk % 2, i, :], ident)
                        last.then_inc(ring_filled, 1)
                    elif e[0] == "exp":
                        _, _, jt, two, step = e
                        i0 = max(jt * P, ib * HALF)
                        n = (ib + 1) * HALF - i0
                        if kk == 0 and jt == 0 and two == 0:
                            pe.wait_ge(one_rows, b + 1)
                        if jt == 0 and two == 0:
                            pe.wait_ge(shift_in, b * (64 * len(blocks)) + 64 * (kk + 1))
                        o = open_unit(b, event_name(e))
                        for i in range(2):
                            last = mm(o[:, i, 0:n], ks[0:3 * DH + 2, jt * P:(jt + 1) * P],
                                      qs[0:3 * DH + 2, 4 * hg + 2 * two + i, i0:i0 + n], start=True, stop=True)
                        last.then_inc(ring_filled, 1)
                    else:
                        _, _, jt, step = e
                        i0 = max(jt * P, ib * HALF)
                        n = (ib + 1) * HALF - i0
                        last_jt = TPH * (ib + 1) - 1
                        if jt == 0:
                            open_unit(b, event_name(e))
                            if hg == 0:
                                wait_read(pe, b, f"L2.vt{ib}")
                        name = event_name(("exp", kk, jt, 1, step))
                        if name in diag_no:
                            pe.wait_ge(diag_masked, b * DIAG + diag_no[name] + 1)
                        else:
                            wait_read(pe, b, name)
                        for bank, w in ((0, v2[:, jt, :]), (1, ones[:, 0:DH])):
                            for a in range(4):
                                last = mm(acc[DH * a:DH * (a + 1), bank, HALF - n:HALF], w,
                                          causal_probs(step, a // 2, n)[:, a % 2, :],
                                          start=jt == 0, stop=jt == last_jt)
                        if jt == last_jt:
                            last.then_inc(ring_filled, 1)

            with pe.Fori(0, B) as b:
                pe.wait_ge(h_lo, b * H_PARTS + 1)
                for i, name in enumerate(("L0.q", "L0.k")):
                    o = open_unit(b, name)
                    for hf in range(NB):
                        last = product(o[:, hf, :], [([w[:, i, c, :] for w in wqk0], [s[:, c, token_half(hf)] for s in h])
                                                     for c in range(CT)])
                    last.then_inc(ring_filled, 1)
                full_attention(b, "L0")
                group_normed(b, "L1")
                causal_layer(b)
                group_normed(b, "L3")

        @block.scalar
        def _(act):
            A = nc.scalar.activation

            act.wait_ge(prep_vecs, 1)
            for l in SPLIT_ORDER:
                wait_loaded(act, l)
                for src, two, idx, g in SPLIT[l]:
                    A(part(two, 0, idx), src, ACT.Identity, scale=g).then_inc(prep_hi, 1)
                if l in OUTPUT_PRODUCT:
                    n, slot_no = OUTPUT_PRODUCT[l]
                    act.wait_ge(prep_mm, n)
                    nc.scalar.copy(wvo[l][0][:, :, :], ring[:, slot_no, :, 0:C]).then_inc(prep_hi, 1)
            act.wait_ge(prep_done, 1)
            nc.scalar.copy(idle_act[:, :], gamma[:, :]).then_inc(act_read, total["act"])

            def hi(b, name, dst, src=None, bias=0.0, scale=1.0):
                wait_filled(act, b, name)
                A(dst, flat(name) if src is None else src, ACT.Identity, bias=bias,
                  scale=scale).then_inc(hi_ready, 1)

            def full_attention(b, l):
                def exp(ti):
                    act.wait_ge(row_max_ready, b * (3 * NT) + LAYER3[l] * NT + ti + 1)
                    if ti >= 2:
                        wait_filled(act, b, f"{l}.t{ti - 2}")
                    A(probs[:, ti % 2, :], flat(f"{l}.s{ti}"), ACT.Exp, bias=neg_max[:, ti:ti + 1],
                      accum_out=row_sum[:, ti:ti + 1]).then_inc(act_read, 1)

                def turned(ti):
                    ts = slice((ti % TPH) * P, (ti % TPH + 1) * P)
                    hi(b, f"{l}.t{ti}", probsT[0][:, ti // TPH, :, ts],
                       slot(f"{l}.t{ti}").rearrange("p b (s n) -> p (b s) n", n=P))

                def values_hi(i):
                    hi(b, f"{l}.v{i}", vt[0][:, i * TPH:(i + 1) * TPH, :].rearrange("p t c -> p (t c)"))

                if l == "L0":
                    values_hi(0)
                else:
                    queries_hi(b, l, 1)
                exp(0)
                exp(1)
                if l != "L0":
                    values_hi(0)
                values_hi(1)
                for ti in range(NT):
                    turned(ti)
                    if ti + 2 < NT:
                        exp(ti + 2)

            def pair_hi(b, name, dst, bias):
                wait_filled(act, b, name)
                for m in range(CT):
                    last = A(dst(m), slot(name)[:, m, :], ACT.Identity, bias=bias(m))
                last.then_inc(hi_ready, 1)

            def token_half(hf):
                return slice(hf * HALF, (hf + 1) * HALF)

            def queries_hi(b, l, hf):
                pair_hi(b, f"{l}.q{hf}", lambda m: q[0][:, m, token_half(hf)], lambda m: bqs[l][:, m:m + 1])

            def keys_hi(b, l, hf):
                pair_hi(b, f"{l}.k{hf}", lambda m: k[0][:, m, token_half(hf)], lambda m: vec(f"{l}_bk", m))

            def group_normed(b, l):
                n = 1 if l == "L1" else 2
                act.wait_ge(gn_coef_ready, b * 2 + n)
                for hf in range(NB):
                    for c in range(CT):
                        last = A(h[0][:, c, token_half(hf)], x[:, c, token_half(hf)], ACT.Identity,
                                 scale=gn_sc[:, c:c + 1], bias=gn_nb[:, c:c + 1])
                    last.then_inc(h_hi, 1)
                queries_hi(b, l, 0)
                keys_hi(b, l, 0)
                keys_hi(b, l, 1)
                full_attention(b, l)

            def stage(b, e):
                kind, hf = e
                if kind not in FILLS:
                    return
                name = event_name(e)
                sl = token_half(hf)
                t0, n = PARTS[hf]
                tokens = slice(t0 * P, (t0 + n) * P)
                cols = slice((t0 % TPH) * P, (t0 % TPH + n) * P)
                if kind == "xt":
                    wait_filled(act, b, name)
                    nc.scalar.copy(xs[:, hf * TPH:(hf + 1) * TPH, :].rearrange("p t c -> p (t c)"),
                                   flat(name)).then_inc(act_read, 1)
                elif kind == "xn":
                    hi(b, name, h[0][:, :, sl], slot(name))
                elif kind == "ta":
                    hi(b, name, hn[0][:, :, cols], slot(name)[:, :, 0:n * P])
                elif kind == "q":
                    pair_hi(b, name, lambda m: q2[0][:, m, sl], lambda m: bq2[:, m:m + 1])
                elif kind == "kv":
                    wait_filled(act, b, name)
                    A(an[3 * DH:P, 2 * hf:2 * hf + 2, :].rearrange("p t c -> p (t c)"), slot(name)[3 * DH:P, 0, :],
                      ACT.Identity, bias=bkv2[3 * DH:P, :])
                    hi(b, name, ks[0:3 * DH, sl], slot(name)[0:3 * DH, 0, :], bias=bkv2[0:3 * DH, :])
                elif kind == "tg":
                    wait_filled(act, b, name)
                    for c in range(CT):
                        last = A(gelu[:, c, tokens], slot(name)[:, c, 0:n * P], ACT.Gelu,
                                 scale=vec("L2_f2_g", c), bias=vec("L2_f2_b", c))
                    last.then_inc(act_read, 1)
                elif kind == "w2":
                    wait_filled(act, b, name)
                    for c in range(CT):
                        last = A(x[:, c, tokens], slot(name)[:, c, 0:n * P], ACT.Identity, bias=vec("L2_b2", c))
                    last.then_inc(act_read, 1)

            def causal_layer(b):
                for e in schedule:
                    if len(e) == 2 and e[0] != "shift":
                        stage(b, e)
                    elif e[0] == "shift":
                        wait_filled(act, b, event_name(e))
                        nc.scalar.copy(max_rows[:, e[1] % 2, :], slot(event_name(e))[:, 0, :]).then_inc(act_read, 1)
                    elif e[0] == "exp":
                        _, kk, jt, two, step = e
                        ib = blocks[kk][1]
                        n = (ib + 1) * HALF - max(jt * P, ib * HALF)
                        wait_filled(act, b, event_name(e))
                        A(causal_probs(step, two, n), slot(event_name(e))[:, :, 0:n],
                          ACT.Exp).then_inc(act_read, 1)
                    elif e[0] == "values" and e[2] == TPH * (blocks[e[1]][1] + 1) - 1:
                        wait_filled(act, b, event_name(e))
                        if e[1]:
                            act.wait_ge(out_ready, b * (2 * len(blocks)) + 2 * e[1])
                        nc.scalar.copy(sums[:, :, :], acc).then_inc(act_read, 1)

            act.wait_ge(x_in, 16)
            nc.scalar.copy(h[0][:, :, :], xin[:, :, :]).then_inc(h_hi, 1)
            with act.Fori(0, B) as b:
                hi(b, "L0.q", qs0[:, :], bias=bqk0[:, 0:1])
                hi(b, "L0.k", ks0[:, :], bias=bqk0[:, 1:2])
                full_attention(b, "L0")
                group_normed(b, "L1")
                stage(b, ("xt", 0))
                stage(b, ("xn", 0))
                causal_layer(b)
                group_normed(b, "L3")
                wait_filled(act, b, f"L3.o0{CT - 1}")
                act.wait_ge(x_in, b * 16 + 32)
                nc.scalar.copy(h[0][:, :, :], xin[:, :, :]).then_inc(h_hi, 1)

        @block.vector
        def _(dve):
            steps = [0]
            v = nc.vector

            def then(b, ins):
                steps[0] += 1
                ins.then_inc(dve_step, 1)
                dve.wait_ge(dve_step, b * DVE_STEPS + steps[0])

            def f32(ap):
                return ap.bitcast(F32)

            wait_loaded(dve, "L0")
            for c in range(CT):
                v.tensor_copy(f1b_wide[:, c, :], vec("L2_f1_b", c).broadcast_to([P, P]))
            v.tensor_copy(mask[:, 0, :], ident)
            v.tensor_copy(mask[:, 1, :], causal)
            bv0 = vecs[:, VECS.index("L0_bv"), :]
            v.tensor_scalar(bv0, bv0, gamma[:, 0:1], None, ALU.mult)
            for l in ("L1", "L3"):
                v.tensor_scalar(bqs[l][:, :], vecs[:, VECS.index(f"{l}_bq"), :], C ** -0.5, None, ALU.mult)
            v.tensor_scalar(ln1_scaled[:, :], vecs[:, VECS.index("L2_ln1_g"), :], DH ** -0.5, None,
                            ALU.mult).then_inc(prep_vecs, 1)
            dve.wait_ge(prep_vecs, 1)
            count = 0
            for l in SPLIT_ORDER:
                for src, two, idx, g in SPLIT[l]:
                    count += 1
                    dve.wait_ge(prep_hi, count)
                    v.scalar_tensor_tensor(out=part(two, 1, idx), in0=src, scalar=g, in1=f32(part(two, 0, idx)),
                                           op0=ALU.mult, op1=ALU.subtract)
                if l in OUTPUT_PRODUCT:
                    count += 1
                    o = ring[:, OUTPUT_PRODUCT[l][1], :, :]
                    dve.wait_ge(prep_hi, count)
                    v.tensor_tensor(bvo[l][:, :], o[:, :, C:C + 1].rearrange("p c o -> p (c o)"),
                                    vecs[:, VECS.index(f"{l}_bo"), :], ALU.add)
                    v.tensor_tensor(wvo[l][1][:, :, :], o[:, :, 0:C], f32(wvo[l][0][:, :, :]), ALU.subtract)
            dve.wait_ge(prep_mm, 3)
            o = ring[:, 1, 0, :]
            v.tensor_scalar(bq2[:, :], o[:, 0:HG], DH ** -0.5, None, ALU.mult)
            v.tensor_copy(bkv2[:, :], o[:, 2:3])
            v.tensor_tensor(rows[:, 2, :], rows[:, 2, :], o[:, C:2 * C], ALU.add).then_inc(prep_done, 1)
            dve.wait_ge(prep_done, 1)
            v.memset(idle_dve[:, 0:1], 0.0).then_inc(dve_read, total["dve"])
            dve.wait_ge(dve_read, total["dve"])

            def lo(b, name, dst, hi, src=None, bias=None, signal=True):
                wait_hi(dve, b, name)
                src = flat(name) if src is None else src
                if bias is None:
                    ins = v.tensor_tensor(dst, src, f32(hi), ALU.subtract)
                else:
                    ins = v.scalar_tensor_tensor(out=dst, in0=src, scalar=bias, in1=f32(hi), op0=ALU.add,
                                                 op1=ALU.subtract)
                if signal:
                    ins.then_inc(dve_read, 1)

            def pair_lo(b, name, dst, hi, bias):
                wait_hi(dve, b, name)
                for m in range(CT):
                    ins = v.scalar_tensor_tensor(out=dst(m), in0=slot(name)[:, m, :], scalar=bias(m), in1=f32(hi(m)),
                                                 op0=ALU.add, op1=ALU.subtract)
                ins.then_inc(dve_read, 1)

            def token_half(hf):
                return slice(hf * HALF, (hf + 1) * HALF)

            def queries_lo(b, l, hf):
                sl = token_half(hf)
                pair_lo(b, f"{l}.q{hf}", lambda m: q[1][:, m, sl], lambda m: q[0][:, m, sl],
                        lambda m: bqs[l][:, m:m + 1])

            def keys_lo(b, l, hf):
                sl = token_half(hf)
                pair_lo(b, f"{l}.k{hf}", lambda m: k[1][:, m, sl], lambda m: k[0][:, m, sl],
                        lambda m: vec(f"{l}_bk", m))

            def full_attention(b, l, base, bias, dst):
                first = b * (3 * NT) + LAYER3[l] * NT

                def row_max(ti):
                    wait_filled(dve, b, f"{l}.s{ti}")
                    v.tensor_reduce(neg_max[:, ti:ti + 1], flat(f"{l}.s{ti}"), AX_X, ALU.max,
                                    negate=True).then_inc(row_max_ready, 1)

                def scale(ti):
                    wait_read(dve, b, f"{l}.s{ti}")
                    then(b, v.reciprocal(row_inv[:, ti:ti + 1], row_sum[:, ti:ti + 1]))
                    v.tensor_scalar(probs[:, ti % 2, :], probs[:, ti % 2, :], row_inv[:, ti:ti + 1],
                                    None, ALU.mult).then_inc(probs_scaled, 1)

                def turned(ti):
                    ts = slice((ti % TPH) * P, (ti % TPH + 1) * P)
                    ap = [s[:, ti // TPH, :, ts] for s in probsT]
                    lo(b, f"{l}.t{ti}", ap[1], ap[0], slot(f"{l}.t{ti}").rearrange("p b (s n) -> p (b s) n", n=P))

                def residual(ib, ct):
                    sl = slice(ib * HALF, (ib + 1) * HALF)
                    wait_filled(dve, b, f"{l}.o{ib}{ct}")
                    v.scalar_tensor_tensor(out=dst[:, ct, sl], in0=acc[:, ct, :], scalar=bias(ct),
                                           in1=base[:, ct, sl], op0=ALU.add, op1=ALU.add).then_inc(dve_read, 1)
                    if l == "L0":
                        wait_read(dve, b, f"{l}.o{ib}{ct}")
                        ins = v.bn_stats(gn_stats[:, ct, ib, :], dst[:, ct, sl])
                        if ib == NB - 1 and ct == CT - 1:
                            then(b, ins)

                def values_lo(i):
                    ap = [s[:, i * TPH:(i + 1) * TPH, :].rearrange("p t c -> p (t c)") for s in vt]
                    lo(b, f"{l}.v{i}", ap[1], ap[0])

                if l != "L0":
                    queries_lo(b, l, 1)
                row_max(0)
                row_max(1)
                for ti in range(NT):
                    scale(ti)
                    if ti:
                        turned(ti - 1)
                    else:
                        values_lo(0)
                    if ti + 2 < NT:
                        row_max(ti + 2)
                    if ti == 0:
                        values_lo(1)
                    if ti == TPH + 2:
                        residual(0, 0)
                turned(NT - 1)
                residual(0, 1)
                if l == "L1":
                    stage(b, ("xt", 0))
                elif l == "L3":
                    split_input(b * 16 + 32, b * H_PARTS + H_PARTS + 1)
                residual(1, 0)
                if l == "L1":
                    stage(b, ("xn", 0))
                residual(1, 1)

            def group_normed(b, l, dst):
                n = 1 if l == "L1" else 2
                r = norm_no[f"{l}.gn"]
                v.memset(idle_dve[:, r:r + 1], 0.0)
                chunks = 2 if l == "L1" else 4
                v.bn_aggr(gn_mv[:, 0, :], gn_stats[:, 0, 0:chunks, :].rearrange("p h s -> p (h s)"))
                then(b, v.bn_aggr(gn_mv[:, 1, :], gn_stats[:, 1, 0:chunks, :].rearrange("p h s -> p (h s)")))
                mean, var = gn_mv[:, :, 0], gn_mv[:, :, 1]
                then(b, v.tensor_tensor(gn_sq[:, :], mean, mean, ALU.mult))
                v.tensor_copy(gn_in[:, :, 0], mean)
                v.tensor_tensor(gn_in[:, :, 1], gn_sq[:, :], var, ALU.add).then_inc(gn_in_ready, 1)
                wait_filled(dve, b, f"{l}.gn")
                v.tensor_copy(gn_out[:, :, :].rearrange("p c s -> p (c s)"),
                              slot(f"{l}.gn")[:, 0, 0:2 * CT]).then_inc(dve_read, 1)
                wait_read(dve, b, f"{l}.gn")
                gmean, gsq = gn_out[:, :, 0], gn_out[:, :, 1]
                then(b, v.tensor_tensor(gn_sq[:, :], gmean, gmean, ALU.mult))
                v.scalar_tensor_tensor(out=var_eps[:, r, 0:CT], in0=gsq, scalar=EPS_GN, in1=gn_sq[:, :],
                                       op0=ALU.add, op1=ALU.subtract).then_inc(var_ready, 1)
                dve.wait_ge(rstd_ready, b * NORMS + r + 1)
                then(b, v.tensor_tensor(gn_sc[:, :], rstd[:, r, 0:CT], vecs[:, VECS.index(f"{l}_g"), :], ALU.mult))
                then(b, v.tensor_tensor(gn_msc[:, :], gmean, gn_sc[:, :], ALU.mult))
                v.tensor_tensor(gn_nb[:, :], vecs[:, VECS.index(f"{l}_b"), :], gn_msc[:, :],
                                ALU.subtract).then_inc(gn_coef_ready, 1)
                dve.wait_ge(gn_coef_ready, b * 2 + n)
                for hf in range(NB):
                    sl = token_half(hf)
                    for c in range(CT):
                        ins = v.tensor_scalar(h_full[:, c, sl], x[:, c, sl], gn_sc[:, c:c + 1], gn_nb[:, c:c + 1],
                                              ALU.mult, ALU.add)
                    then(b, ins)
                    dve.wait_ge(h_hi, b * H_PARTS + 2 * n + hf)
                    v.tensor_tensor(h[1][:, :, sl], h_full[:, :, sl], f32(h[0][:, :, sl]),
                                    ALU.subtract).then_inc(h_lo, 1)
                queries_lo(b, l, 0)
                if l == "L1":
                    dve.wait_ge(y_free, b + 1)
                keys_lo(b, l, 0)
                keys_lo(b, l, 1)
                full_attention(b, l, x, lambda ct: bvo[l][:, ct:ct + 1], dst)

            def norm_start(b, name, src, t0, n, dst=None, gain=None):
                r = norm_no[name]
                for i in range(n):
                    ins = v.bn_stats(ln_stats[:, r, i, :], src[:, t0 + i, :])
                then(b, ins)
                v.memset(idle_dve[:, r:r + 1], 0.0)
                for i in range(n):
                    ins = v.bn_aggr(ln_mv[:, r, i, :], ln_stats[:, r, i, :])
                then(b, ins)
                v.tensor_scalar(var_eps[:, r, 0:n], ln_mv[:, r, 0:n, 1], EPS_LN, None, ALU.add).then_inc(var_ready, 1)
                if gain is not None:
                    for i in range(n):
                        ins = v.scalar_tensor_tensor(out=dst[:, t0 + i, :], in0=src[:, t0 + i, :],
                                                     scalar=ln_mv[:, r, i, 0:1], in1=gain,
                                                     op0=ALU.subtract, op1=ALU.mult)
                    then(b, ins)

            def norm_end(b, name, src, t0, n, dst, shift=None):
                r = norm_no[name]
                dve.wait_ge(rstd_ready, b * NORMS + r + 1)
                for i in range(n):
                    if shift is None:
                        ins = v.tensor_scalar(dst[:, t0 + i, :], src[:, t0 + i, :], ln_mv[:, r, i, 0:1],
                                              rstd[:, r, i:i + 1], ALU.subtract, ALU.mult)
                    else:
                        ins = v.scalar_tensor_tensor(out=dst[:, t0 + i, :], in0=src[:, t0 + i, :],
                                                     scalar=rstd[:, r, i:i + 1], in1=shift, op0=ALU.mult, op1=ALU.add)
                if shift is None:
                    ins.then_inc(ln_ready, 1)
                else:
                    then(b, ins)

            def stage(b, e):
                kind, hf = e
                name = event_name(e)
                sl = token_half(hf)
                t0, n = PARTS[hf]
                ts = slice(t0, t0 + n)
                tokens = slice(t0 * P, (t0 + n) * P)
                cols = slice((t0 % TPH) * P, (t0 % TPH + n) * P)
                if kind in FILLS:
                    tiles = slot(name).rearrange("p b (s c) -> p (b s) c", c=C)[:, 0:n, :]
                if kind == "xt":
                    if hf == 0:
                        v.memset(ks[3 * DH:3 * DH + 2, :].bitcast(F32), 1.0).then_inc(one_rows, 1)
                    wait_read(dve, b, name)
                    norm_start(b, f"L2.ln1.{hf}", xs, hf * TPH, TPH)
                    norm_end(b, f"L2.ln1.{hf}", xs, hf * TPH, TPH, an)
                elif kind == "xn":
                    lo(b, name, h[1][:, :, sl], h[0][:, :, sl], slot(name))
                elif kind == "q":
                    pair_lo(b, name, lambda m: q2[1][:, m, sl], lambda m: q2[0][:, m, sl],
                            lambda m: bq2[:, m:m + 1])
                elif kind == "kv":
                    kv = slot(name)[:, 0, :]
                    wait_hi(dve, b, name)
                    lo(b, name, ks[DH:2 * DH, sl], ks[DH:2 * DH, sl], kv[DH:2 * DH, :], bias=bkv2[DH:2 * DH, :])
                elif kind == "vt":
                    wait_filled(dve, b, name)
                    v.tensor_copy(v2[:, hf * TPH:(hf + 1) * TPH, :], slot(name)[:, 0, :].rearrange("p (s n) -> p s n", n=P)[:, :, 3 * DH:P]
                                  ).then_inc(dve_read, 1)
                elif kind == "wo":
                    wait_filled(dve, b, name)
                    v.tensor_tensor(xs[:, ts, :], tiles, xs[:, ts, :], ALU.add).then_inc(dve_read, 1)
                    wait_read(dve, b, name)
                    norm_start(b, f"L2.ln2.{hf}", xs, t0, n, xs, rows[:, 0, :])
                elif kind == "ln2b":
                    norm_end(b, f"L2.ln2.{hf}", xs, t0, n, xs, rows[:, 1, :])
                    norm_start(b, f"L2.f1.{hf}", xs, t0, n)
                elif kind == "f1b":
                    norm_end(b, f"L2.f1.{hf}", xs, t0, n, an)
                elif kind == "ta":
                    lo(b, name, hn[1][:, :, cols], hn[0][:, :, cols], slot(name)[:, :, 0:n * P])
                elif kind == "w1":
                    wait_filled(dve, b, name)
                    v.tensor_tensor(an[:, ts, :], tiles, rows[:, 2, :].unsqueeze(1).broadcast_to([P, n, C]),
                                    ALU.add).then_inc(dve_read, 1)
                    wait_read(dve, b, name)
                    norm_start(b, f"L2.f2.{hf}", an, t0, n)
                elif kind == "f2b":
                    norm_end(b, f"L2.f2.{hf}", an, t0, n, an)
                elif kind == "tg":
                    wait_read(dve, b, name)
                    then(b, v.tensor_copy(act2[0][:, :, cols], gelu[:, :, tokens]))
                    v.tensor_tensor(act2[1][:, :, cols], gelu[:, :, tokens], f32(act2[0][:, :, cols]),
                                    ALU.subtract).then_inc(act2_ready, 1)
                elif kind == "w2":
                    wait_read(dve, b, name)
                    for c in range(CT):
                        for i in range(t0, t0 + n, 2):
                            ins = v.bn_stats(gn_stats[:, c, i // 2, :], x[:, c, i * P:(i + 2) * P])
                    if hf == len(PARTS) - 1:
                        then(b, ins)

            def causal_layer(b):
                for e in schedule:
                    if len(e) == 2 and e[0] != "shift":
                        stage(b, e)
                    elif e[0] == "max":
                        _, kk, ti, ch, lo_key, hi_key, two = e
                        n = hi_key - lo_key
                        name = event_name(e)
                        i = ti % TPH
                        cols = cmax[:, kk % 2, i, 2 * two:2 * two + 2]
                        parts = part_max[:, i, :, 2 * two:2 * two + 2]
                        wait_filled(dve, b, name)
                        v.tensor_reduce(cols if ti < TPH else parts[:, ch, :], slot(name)[:, :, 0:n], AX_X,
                                        ALU.max, negate=True).then_inc(dve_read, 1)
                        if ch == 1:
                            wait_read(dve, b, name)
                            ins = v.tensor_tensor(cols, parts[:, 0, :], parts[:, 1, :], ALU.min)
                            if i == TPH - 1 and two == 1:
                                then(b, ins)
                        if e == last_max[kk]:
                            wait_read(dve, b, name)
                            s = kk % 2
                            then(b, v.tensor_copy(cmax_hi[:, s, :, :], cmax[:, s, :, :]))
                            v.tensor_copy(max_cols[:, s, :, 0:P:DH], f32(cmax_hi[:, s, :, :]))
                            v.tensor_tensor(max_cols[:, s, :, 1:P:DH], cmax[:, s, :, :], f32(cmax_hi[:, s, :, :]),
                                            ALU.subtract).then_inc(max_ready, 1)
                    elif e[0] == "norm":
                        _, kk, piece = e
                        hg, ib = blocks[kk]
                        sl = token_half(ib)
                        if piece == 0:
                            wait_read(dve, b, f"L2.o{kk}")
                        half, what = divmod(piece, 3)
                        if what < 2:
                            at = half * 2 * P + what * P
                            ins = v.reciprocal(sums[:, 1, at:at + P], sums[:, 1, at:at + P])
                            if what:
                                then(b, ins)
                        else:
                            cs = slice(half * 2 * P, (half + 1) * 2 * P)
                            to = slice(ib * HALF + cs.start, ib * HALF + cs.stop)
                            then(b, v.tensor_tensor(sums[:, 0, cs], sums[:, 0, cs], sums[:, 1, cs], ALU.mult))
                            then(b, v.tensor_copy(heads_out[0][:, hg, to], sums[:, 0, cs]))
                            v.tensor_tensor(heads_out[1][:, hg, to], sums[:, 0, cs], f32(heads_out[0][:, hg, to]),
                                            ALU.subtract).then_inc(out_ready, 1)

            def split_input(arrived, nth):
                dve.wait_ge(x_in, arrived)
                dve.wait_ge(h_hi, nth)
                v.tensor_tensor(h[1][:, :, :], xin[:, :, :], f32(h[0][:, :, :]), ALU.subtract).then_inc(h_lo, 1)

            split_input(16, 1)
            with dve.Fori(0, B) as b:
                steps[0] = 0
                gs = slice(2 * DH, 3 * DH)
                lo(b, "L0.q", qs0[gs, :], qs0[gs, :], flat("L0.q")[gs, :], bias=bqk0[gs, 0:1])
                gs = slice(DH, 2 * DH)
                lo(b, "L0.k", ks0[gs, :], ks0[gs, :], flat("L0.k")[gs, :], bias=bqk0[gs, 1:2])
                full_attention(b, "L0", xin, lambda ct: bv0[:, ct:ct + 1], x)
                group_normed(b, "L1", x)
                causal_layer(b)
                group_normed(b, "L3", y)
            assert steps[0] == DVE_STEPS, steps[0]


def kernel(**inputs):
    import numpy as _np
    import concourse.bacc as _bacc
    from concourse import mybir as _mybir
    from concourse.bass_utils import run_bass_kernel_spmd as _run

    i = {n: _np.asarray(a) for n, a in inputs.items()}
    cols = [i["L0_conv_bv"]] + [i[f"L1_conv_{n}"] for n in ("gn_scale", "gn_bias", "bq", "bk", "bv", "bo")]
    cols += [i[f"L2_conv_{n}"] for n in ("ln1_g", "ln1_b", "ff_ln1_g", "ff_ln1_b", "ff_ln2_g", "ff_ln2_b", "ff_b2")]
    cols += [i[f"L3_conv_{n}"] for n in ("norm_g", "norm_b", "bq", "bk", "bv", "bo")]
    group = C // 32
    channel = _np.arange(P)
    consts = _np.stack([
        _np.eye(P, dtype=_np.float32),
        (channel[:, None] // group == channel[None, :] // group).astype(_np.float32) / _np.float32(group),
        _np.where(channel[None, :] > channel[:, None], _np.float32(-3e38), _np.float32(0)),
    ])
    arrays = {
        "x": i["x"],
        "L0_WqkT": _np.stack([_np.tile(i[f"L0_conv_W{w}"].T, (1, 4)) for w in "qk"]),
        "L0_bqk": _np.stack([_np.tile(i[f"L0_conv_b{w}"], 4) for w in "qk"], axis=1),
        "L0_WvT": i["L0_conv_Wv"].T,
        "gamma": i["L0_conv_gamma"],
        "vecs": _np.stack(cols).reshape(len(VECS), CT, P).transpose(2, 0, 1),
        "rows": _np.stack([i["L2_conv_ln2_g"], i["L2_conv_ln2_b"], i["L2_conv_ff_b1"]]),
        "consts": consts.transpose(1, 0, 2),
        "L2_wq": i["L2_conv_wq"], 
        "L2_wkv": _np.concatenate([i["L2_conv_wkv"][:, :DH]] * 3 + [i["L2_conv_wkv"][:, DH:]], axis=1),
        "L2_wo": i["L2_conv_wo"],
        "L2_w1": i["L2_conv_ff_w1"], "L2_w2": i["L2_conv_ff_w2"],
    }
    for l in ("L1", "L3"):
        arrays[f"{l}_wqT"] = i[f"{l}_conv_wq"].T
        arrays[f"{l}_wkT"] = i[f"{l}_conv_wk"].T
        arrays[f"{l}_wv"] = i[f"{l}_conv_wv"]
        arrays[f"{l}_woT"] = i[f"{l}_conv_wo"].T
    arrays = {f"{n}_dram": _np.ascontiguousarray(a) for n, a in arrays.items()}
    nc = _bacc.Bacc("TRN2", target_bir_lowering=False, num_devices=1)
    tensors = {n[:-5]: nc.dram_tensor(n, a.shape, _mybir.dt.from_np(a.dtype), kind="ExternalInput").ap()
               for n, a in arrays.items()}
    tensors["out"] = nc.dram_tensor("out_dram", (B, C, 32, 32), _mybir.dt.float32, kind="ExternalOutput").ap()
    build(nc, tensors)
    r = _run(nc, [arrays], core_ids=[0])
    return r.results[0]["out_dram"]
```
